# Optimizing a Trainium2 kernel written in Bass

```python
import numpy as np
import jax
import jax.numpy as jnp

def _softmax(x, axis=-1):
    return jax.nn.softmax(x, axis=axis)

def _gelu(x):
    return jax.nn.gelu(x, approximate=True)

def _silu(x):
    return jax.nn.silu(x)

def _sigmoid(x):
    return jax.nn.sigmoid(x)

def _layernorm(x, axis=-1, eps=1e-05):
    m = jnp.mean(x, axis=axis, keepdims=True)
    v = jnp.var(x, axis=axis, keepdims=True)
    return (x - m) / jnp.sqrt(v + eps)

def _scatter_add(tgt, idx, src, axis=0):
    return tgt.at[idx].add(src)

def _segment_sum(src, seg, n):
    return jax.ops.segment_sum(src, seg, n)
kernel_name = 'mk_gnn_resnorm_d2_gnn_r32_22d7ca'

def setup_inputs(seed: int=0):
    np.random.seed(seed)
    _w = jnp.asarray

    def _rec_inputs():
        import jax
        import jax.numpy as jnp
        _gk = jax.random.key(seed)
        x = -7.329e-05 + 0.9999 * jax.random.normal(jax.random.fold_in(_gk, 1), (10000, 512), jnp.float32)
        src = jax.random.randint(jax.random.fold_in(_gk, 2), (10000,), 0, 10000, jnp.int32)
        dst = jax.random.randint(jax.random.fold_in(_gk, 3), (10000,), 0, 10000, jnp.int32)
        _o = jnp.argsort(dst, stable=True)
        src = src[_o]
        dst = dst[_o]
        edge_attr_20 = jax.random.uniform(jax.random.fold_in(_gk, 12), (10000, 20), jnp.float32, 0.0, 0.999999)
        edge_attr_3 = -0.0005747 + 0.998114 * jax.random.normal(jax.random.fold_in(_gk, 13), (10000, 3), jnp.float32)
        edge_weight = jax.random.uniform(jax.random.fold_in(_gk, 15), (10000,), jnp.float32, 0.0, 0.999998)
        return (x, src, dst, edge_attr_20, edge_attr_3, edge_weight)
    x, src, dst, edge_attr_20, edge_attr_3, edge_weight = _rec_inputs()

    def _L0_gnn_setup():
        import jax, jax.numpy as jnp
        import numpy as np
        N_NODES = 3125
        N_EDGES = 15625
        D_IN = 512
        D_OUT = 512
        key = jax.random.key(seed)
        k1, k2, k3, k4 = jax.random.split(key, 4)
        x = jax.random.normal(k1, (N_NODES, D_IN), dtype=jnp.float32)
        edge_weight = jax.random.uniform(k2, (N_EDGES,), dtype=jnp.float32)
        W = jax.random.normal(k3, (D_IN, D_OUT), dtype=jnp.float32) * (1.0 / np.sqrt(D_IN))
        b = jnp.zeros((D_OUT,), dtype=jnp.float32)
        edge_index = jax.random.randint(k4, (2, N_EDGES), 0, N_NODES, dtype=jnp.int32)
        return {'x': x, 'edge_weight': edge_weight, 'W': W, 'b': b, 'edge_index': edge_index}
    _L0_gnn_all = _L0_gnn_setup()
    _L0_gnn_in = {k: v for k, v in _L0_gnn_all.items() if k in ('W', 'b')}
    del _L0_gnn_all

    def _L1_gnn_setup():
        import jax, jax.numpy as jnp
        import numpy as np
        N_ATOMS = 5000
        N_EDGES = 50000
        C = 128
        F = 128
        N_RBF = 20
        LOG2 = float(np.log(2.0))
        Y0 = float(1.0 / np.sqrt(4.0 * np.pi))
        Y1_SCALE = float(np.sqrt(3.0 / (4.0 * np.pi)))

        def shifted_softplus(x):
            return jax.nn.softplus(x) - LOG2

        def _forward(x, idx_i, idx_j, f_ij, rcut_ij, r_ij, W_in2f_s, W_in2f_v, Wf1, bf1, Wf2, bf2, W1_s, W1_v, W2_s, W2_v):
            n = x.shape[0]
            e = r_ij.shape[0]
            xs = x[:, :C] @ (W_in2f_s / np.sqrt(C))
            xv = jnp.einsum('nci,cf->nfi', x[:, C:].reshape(n, C, 3), W_in2f_v) / np.sqrt(C)
            sj = xs[idx_j]
            vj = xv[idx_j]
            u = r_ij / jnp.linalg.norm(r_ij, axis=-1, keepdims=True)
            Yv = Y1_SCALE * u
            o0a = sj * Y0
            o0b = jnp.einsum('efi,ei->ef', vj, Yv) / np.sqrt(3.0)
            s2 = jnp.stack([o0a, o0b], axis=-1).reshape(e, 2 * F)
            ova = sj[:, :, None] * Yv[:, None, :]
            ovb = vj * Y0
            v2 = jnp.stack([ova, ovb], axis=2)
            w1 = jnp.cross(vj, Yv[:, None, :]) / np.sqrt(2.0)
            ax, ay, az = (vj[..., 0], vj[..., 1], vj[..., 2])
            bx, by, bz = (Yv[:, None, 0], Yv[:, None, 1], Yv[:, None, 2])
            t = jnp.stack([(ax * by + ay * bx) / np.sqrt(2.0), (ay * bz + az * by) / np.sqrt(2.0), (2.0 * az * bz - ax * bx - ay * by) / np.sqrt(6.0), (az * bx + ax * bz) / np.sqrt(2.0), (ax * bx - ay * by) / np.sqrt(2.0)], axis=-1)
            h = shifted_softplus(f_ij @ Wf1 + bf1)
            W = (h @ Wf2 + bf2) * rcut_ij[:, None]
            m_s = s2 * W[:, :2 * F]
            m_v = (v2.reshape(e, 2 * F, 3) * W[:, 2 * F:4 * F, None]).reshape(e, 6 * F)
            m_w = (w1 * W[:, 4 * F:5 * F, None]).reshape(e, 3 * F)
            m_t = (t * W[:, 5 * F:6 * F, None]).reshape(e, 5 * F)
            x_ij = jnp.concatenate([m_s, m_v, m_w, m_t], axis=1)
            agg = jax.ops.segment_sum(x_ij, idx_i, num_segments=n)
            S = agg[:, :2 * F] @ (W1_s / np.sqrt(2 * F))
            V = jnp.einsum('nmi,mc->nci', agg[:, 2 * F:8 * F].reshape(n, 2 * F, 3), W1_v) / np.sqrt(2 * F)
            S = shifted_softplus(S)
            S = S @ (W2_s / np.sqrt(C))
            V = jnp.einsum('nci,cd->ndi', V, W2_v) / np.sqrt(C)
            return jnp.concatenate([S, V.reshape(n, 3 * C)], axis=1)
        key = jax.random.key(seed)
        ks = jax.random.split(key, 16)
        f32 = jnp.float32
        x = jax.random.normal(ks[0], (N_ATOMS, 4 * C), f32)
        idx_i = jnp.sort(jax.random.randint(ks[1], (N_EDGES,), 0, N_ATOMS))
        idx_j = jax.random.randint(ks[2], (N_EDGES,), 0, N_ATOMS)
        f_ij = jax.random.uniform(ks[3], (N_EDGES, N_RBF), f32)
        rcut_ij = jax.random.uniform(ks[4], (N_EDGES,), f32)
        r_ij = jax.random.normal(ks[5], (N_EDGES, 3), f32)
        W_in2f_s = jax.random.normal(ks[6], (C, F), f32)
        W_in2f_v = jax.random.normal(ks[7], (C, F), f32)
        Wf1 = jax.random.normal(ks[8], (N_RBF, F), f32) / np.sqrt(N_RBF)
        bf1 = 0.1 * jax.random.normal(ks[9], (F,), f32)
        Wf2 = jax.random.normal(ks[10], (F, 6 * F), f32) / np.sqrt(F)
        bf2 = 0.1 * jax.random.normal(ks[11], (6 * F,), f32)
        W1_s = jax.random.normal(ks[12], (2 * F, C), f32)
        W1_v = jax.random.normal(ks[13], (2 * F, C), f32)
        W2_s = jax.random.normal(ks[14], (C, C), f32)
        W2_v = jax.random.normal(ks[15], (C, C), f32)
        return dict(x=x, idx_i=idx_i, idx_j=idx_j, f_ij=f_ij, rcut_ij=rcut_ij, r_ij=r_ij, W_in2f_s=W_in2f_s, W_in2f_v=W_in2f_v, Wf1=Wf1, bf1=bf1, Wf2=Wf2, bf2=bf2, W1_s=W1_s, W1_v=W1_v, W2_s=W2_s, W2_v=W2_v)
    _L1_gnn_all = _L1_gnn_setup()
    _L1_gnn_in = {k: v for k, v in _L1_gnn_all.items() if k in ('W_in2f_s', 'W_in2f_v', 'Wf1', 'bf1', 'Wf2', 'bf2', 'W1_s', 'W1_v', 'W2_s', 'W2_v')}
    del _L1_gnn_all
    return {'x': x, 'src': src, 'dst': dst, 'edge_attr_20': edge_attr_20, 'edge_attr_3': edge_attr_3, 'edge_weight': edge_weight, 'L0_gnn_W': _L0_gnn_in['W'], 'L0_gnn_b': _L0_gnn_in['b'], 'L1_gnn_W_in2f_s': _L1_gnn_in['W_in2f_s'], 'L1_gnn_W_in2f_v': _L1_gnn_in['W_in2f_v'], 'L1_gnn_Wf1': _L1_gnn_in['Wf1'], 'L1_gnn_bf1': _L1_gnn_in['bf1'], 'L1_gnn_Wf2': _L1_gnn_in['Wf2'], 'L1_gnn_bf2': _L1_gnn_in['bf2'], 'L1_gnn_W1_s': _L1_gnn_in['W1_s'], 'L1_gnn_W1_v': _L1_gnn_in['W1_v'], 'L1_gnn_W2_s': _L1_gnn_in['W2_s'], 'L1_gnn_W2_v': _L1_gnn_in['W2_v']}

def reference(x, src, dst, edge_attr_20, edge_attr_3, edge_weight, L0_gnn_W, L0_gnn_b, L1_gnn_W_in2f_s, L1_gnn_W_in2f_v, L1_gnn_Wf1, L1_gnn_bf1, L1_gnn_Wf2, L1_gnn_bf2, L1_gnn_W1_s, L1_gnn_W1_v, L1_gnn_W2_s, L1_gnn_W2_v):
    import jax
    import jax.numpy as jnp

    def _L0_gnn_ref(x, edge_weight, W, b, edge_index):
        import jax, jax.numpy as jnp
        import numpy as np
        N_NODES = 3125
        N_EDGES = 15625
        D_IN = 512
        D_OUT = 512
        N = x.shape[0]
        src, dst = (edge_index[0], edge_index[1])
        loop = jnp.arange(N, dtype=edge_index.dtype)
        src_all = jnp.concatenate([src, loop])
        dst_all = jnp.concatenate([dst, loop])
        w_all = jnp.concatenate([edge_weight, jnp.ones((N,), dtype=x.dtype)])
        deg = jax.ops.segment_sum(w_all, dst_all, num_segments=N)
        deg_inv_sqrt = jnp.where(deg > 0, jax.lax.rsqrt(deg), 0.0)
        norm = deg_inv_sqrt[src_all] * w_all * deg_inv_sqrt[dst_all]
        xp = x @ W
        msg = xp[src_all] * norm[:, None]
        out = jax.ops.segment_sum(msg, dst_all, num_segments=N)
        out = out + b
        return jax.nn.relu(out)

    def _L1_gnn_ref(x, idx_i, idx_j, f_ij, rcut_ij, r_ij, W_in2f_s, W_in2f_v, Wf1, bf1, Wf2, bf2, W1_s, W1_v, W2_s, W2_v):
        import jax, jax.numpy as jnp
        import numpy as np
        N_ATOMS = 5000
        N_EDGES = 50000
        C = 128
        F = 128
        N_RBF = 20
        LOG2 = float(np.log(2.0))
        Y0 = float(1.0 / np.sqrt(4.0 * np.pi))
        Y1_SCALE = float(np.sqrt(3.0 / (4.0 * np.pi)))

        def shifted_softplus(x):
            return jax.nn.softplus(x) - LOG2

        def _forward(x, idx_i, idx_j, f_ij, rcut_ij, r_ij, W_in2f_s, W_in2f_v, Wf1, bf1, Wf2, bf2, W1_s, W1_v, W2_s, W2_v):
            n = x.shape[0]
            e = r_ij.shape[0]
            xs = x[:, :C] @ (W_in2f_s / np.sqrt(C))
            xv = jnp.einsum('nci,cf->nfi', x[:, C:].reshape(n, C, 3), W_in2f_v) / np.sqrt(C)
            sj = xs[idx_j]
            vj = xv[idx_j]
            u = r_ij / jnp.linalg.norm(r_ij, axis=-1, keepdims=True)
            Yv = Y1_SCALE * u
            o0a = sj * Y0
            o0b = jnp.einsum('efi,ei->ef', vj, Yv) / np.sqrt(3.0)
            s2 = jnp.stack([o0a, o0b], axis=-1).reshape(e, 2 * F)
            ova = sj[:, :, None] * Yv[:, None, :]
            ovb = vj * Y0
            v2 = jnp.stack([ova, ovb], axis=2)
            w1 = jnp.cross(vj, Yv[:, None, :]) / np.sqrt(2.0)
            ax, ay, az = (vj[..., 0], vj[..., 1], vj[..., 2])
            bx, by, bz = (Yv[:, None, 0], Yv[:, None, 1], Yv[:, None, 2])
            t = jnp.stack([(ax * by + ay * bx) / np.sqrt(2.0), (ay * bz + az * by) / np.sqrt(2.0), (2.0 * az * bz - ax * bx - ay * by) / np.sqrt(6.0), (az * bx + ax * bz) / np.sqrt(2.0), (ax * bx - ay * by) / np.sqrt(2.0)], axis=-1)
            h = shifted_softplus(f_ij @ Wf1 + bf1)
            W = (h @ Wf2 + bf2) * rcut_ij[:, None]
            m_s = s2 * W[:, :2 * F]
            m_v = (v2.reshape(e, 2 * F, 3) * W[:, 2 * F:4 * F, None]).reshape(e, 6 * F)
            m_w = (w1 * W[:, 4 * F:5 * F, None]).reshape(e, 3 * F)
            m_t = (t * W[:, 5 * F:6 * F, None]).reshape(e, 5 * F)
            x_ij = jnp.concatenate([m_s, m_v, m_w, m_t], axis=1)
            agg = jax.ops.segment_sum(x_ij, idx_i, num_segments=n)
            S = agg[:, :2 * F] @ (W1_s / np.sqrt(2 * F))
            V = jnp.einsum('nmi,mc->nci', agg[:, 2 * F:8 * F].reshape(n, 2 * F, 3), W1_v) / np.sqrt(2 * F)
            S = shifted_softplus(S)
            S = S @ (W2_s / np.sqrt(C))
            V = jnp.einsum('nci,cd->ndi', V, W2_v) / np.sqrt(C)
            return jnp.concatenate([S, V.reshape(n, 3 * C)], axis=1)
        return _forward(x, idx_i, idx_j, f_ij, rcut_ij, r_ij, W_in2f_s, W_in2f_v, Wf1, bf1, Wf2, bf2, W1_s, W1_v, W2_s, W2_v)
    edge_index = jnp.stack([src, dst])
    x = _layernorm(x + _L0_gnn_ref(x, edge_weight, L0_gnn_W, L0_gnn_b, edge_index), axis=-1)
    x = _layernorm(x + _L1_gnn_ref(x, src, dst, edge_attr_20, edge_weight, edge_attr_3, L1_gnn_W_in2f_s, L1_gnn_W_in2f_v, L1_gnn_Wf1, L1_gnn_bf1, L1_gnn_Wf2, L1_gnn_bf2, L1_gnn_W1_s, L1_gnn_W1_v, L1_gnn_W2_s, L1_gnn_W2_v), axis=-1)
    return x

_drawn_inputs = setup_inputs


def setup_inputs(seed=0):
    import zlib

    import numpy as np

    out = dict(_drawn_inputs(seed))
    spreads = {'L0_gnn_b': (0.0, 0.1)}
    factors = {'L1_gnn_bf1': 6.906, 'L1_gnn_bf2': 3.867, 'L1_gnn_W1_s': 4.105, 'L1_gnn_W2_s': 4.09}
    for name, (base, spread) in spreads.items():
        noise = np.random.default_rng([zlib.crc32(name.encode()), seed]).standard_normal(out[name].shape)
        drawn = base * np.exp(spread * noise) if base else spread * noise
        out[name] = jnp.asarray(drawn.astype(out[name].dtype))
    for name, factor in factors.items():
        out[name] = (out[name] * factor).astype(out[name].dtype)
    return out
```

```python
from contextlib import ExitStack

import numpy as np

import concourse.bass as bass
from concourse import mybir

F32 = mybir.dt.float32
I32 = mybir.dt.int32
ALU = mybir.AluOpType
ACT = mybir.ActivationFunctionType

P = 128
N = 10000
T = 80
NP = T * P
D = 512
C = 128
RBF = 20
TRASH = 2 * P
EPS = 1e-5
LOG2 = float(np.log(2.0))
Y0 = float(1.0 / np.sqrt(4.0 * np.pi))
Y1 = float(np.sqrt(3.0 / (4.0 * np.pi)))


def skewed(eng, step, tail, lead, unroll=2):
    steps = T
    for s in range(lead):
        step(s, s % unroll)
    with eng.Fori(lead // unroll, steps // unroll) as j:
        for u in range(unroll):
            step(j * unroll + u, u)
    for s in range(steps, steps + tail):
        step(s, s % unroll)


def live(s, lag):
    return not isinstance(s, int) or 0 <= s - lag < T


def turn(t, slot, n):
    return t // n if isinstance(t, int) else (t - slot) // n


def wait(eng, sem, value):
    if not isinstance(value, int) or value > 0:
        eng.wait_ge(sem, value)


class Stage:

    def __init__(self, sem, t, total):
        self.sem, self.t, self.total, self.n = sem, t, total, 0

    def mark(self, ins):
        self.n += 1
        ins.then_inc(self.sem, 1)

    def reached(self):
        return self.t * self.total + self.n

    def settle(self, eng):
        eng.wait_ge(self.sem, self.reached())


def rows(dram, t):
    return dram[bass.ds(t * P, P), :]


def build(nc, x, src_cols, dst_cols, src_row, dst_row, weight, rbf, vec,
          W0, b0, Win_s, Win_v, Wf1, bf1, Wf2, bf2, W1_s, W1_v, W2_s, W2_v, out):
    sum0 = nc.dram_tensor("sum0", (NP + TRASH, D), F32, kind="Internal").ap()
    sum1 = nc.dram_tensor("sum1", (NP + TRASH, D), F32, kind="Internal").ap()
    x1_d = nc.dram_tensor("x1_d", (NP, D), F32, kind="Internal").ap()

    with ExitStack() as ctx:
        def sb(name, shape, dt=F32):
            return ctx.enter_context(nc.sbuf_tensor(name, shape, dt))

        def sem(name):
            return ctx.enter_context(nc.semaphore(name))

        def ring(name, n, shape, dt=F32):
            return [sb(f"{name}{i}", shape, dt) for i in range(n)]

        bank = [ctx.enter_context(nc.psum_tensor(f"bank{i}", [P, 512], F32)) for i in range(8)]

        zeros = sb("zeros", [P, 1024])
        ident_i = sb("ident_i", [P, P], I32)
        iota_f = sb("iota_f", [P, 256])
        iota_i = sb("iota_i", [P, 256], I32)
        lane_i = sb("lane_i", [P, 2], I32)
        lane = sb("lane", [P, 2])
        trash_i = sb("trash_i", [P, T], I32)
        ident = sb("ident", [P, P])
        before = sb("before", [P, 2, 256])
        src_i = sb("src_i", [P, T], I32)
        dst_i = sb("dst_i", [P, T], I32)
        part_i = sb("part_i", [P, 4, T], I32)
        part = sb("part", [P, 4, T])
        src_f = sb("src_f", [P, T])
        dst_f = sb("dst_f", [P, T])
        trash = sb("trash", [P, T])
        to_trash_src = sb("to_trash_src", [P, T])
        to_trash_dst = sb("to_trash_dst", [P, T])
        ew = sb("ew", [P, T])
        coef = sb("coef", [P, T])
        dsrc = sb("dsrc", [P, T])
        deg = sb("deg", [P, T])
        degm = sb("degm", [P, T])
        degs = sb("degs", [P, T])
        degt = sb("degt", [P, T])
        dis = sb("dis", [P, T])
        rij = sb("rij", [P, T, 3])
        rsq = sb("rsq", [P, T, 3])
        rn = sb("rn", [P, T])
        Y = sb("Y", [P, T, 3])
        W0_s = sb("W0_s", [P, 4, D])
        b0_s = sb("b0_s", [P, D])
        Wins = sb("Wins", [P, C])
        Winv = sb("Winv", [P, C])
        Wf1_s = sb("Wf1_s", [RBF, C])
        bf1_c = sb("bf1_c", [P, 1])
        Wf2_s = sb("Wf2_s", [P, 512])
        bf2_c = sb("bf2_c", [P, 4])
        W1s_r = sb("W1s_r", [P, 2, C])
        W1v_r = sb("W1v_r", [P, 2, C])
        W1s_s = sb("W1s_s", [P, 2, C])
        W1vT = sb("W1vT", [P, 2, C])
        MV = sb("MV", [P, 2, C])
        W2s_r = sb("W2s_r", [P, C])
        W2s_s = sb("W2s_s", [P, C])
        W2v_r = sb("W2v_r", [P, C])

        hot_lo = ring("hot_lo", 2, [P, P])
        hot_hi = ring("hot_hi", 2, [P, T])
        srow = ring("srow", 2, [P, 512], I32)
        slow = ring("slow", 2, [P, 512], I32)
        hotT = ring("hotT", 2, [P, 512])
        junk80 = sb("junk80", [P, 8, T])
        trow = ring("trow", 2, [P, 256], I32)
        G = ring("G", 4, [P, D])
        M = ring("M", 4, [P, 256])
        R = ring("R", 4, [P, D])
        gidx = ring("gidx", 4, [P, 1], I32)
        sidx = ring("sidx", 4, [P, 1], I32)
        junk = ring("junk", 4, [P, 256])
        dup = ring("dup", 4, [P, 1])
        off = ring("off", 4, [P, 1])
        sl = ring("sl", 2, [P, D])
        xl = ring("xl", 2, [P, D])
        zl = ring("zl", 2, [P, D])
        zT = ring("zT", 2, [P, D])
        pre = ring("pre", 2, [P, D])
        res = ring("res", 2, [P, D])
        x1 = ring("x1", 2, [P, D])
        stat = ring("stat", 2, [P, 6])
        mv = ring("mv", 2, [P, 2])
        tiny = ring("tiny", 2, [P, 8])
        trow3 = ring("trow3", 2, [P, P], I32)
        fT = ring("fT", 2, [RBF, P])
        G3 = ring("G3", 2, [P, D])
        proj = ring("proj", 2, [P, P])
        rawT = ring("rawT", 2, [P, 640])
        hx = ring("hx", 2, [P, 3, P])
        hr = ring("hr", 2, [P, P])
        h = ring("h", 2, [P, P])
        feat = ring("feat", 2, [P, 640])
        m = ring("m", 2, [P, 768])
        msg = ring("msg", 2, [P, 640])
        M3 = ring("M3", 2, [P, P])
        R3 = ring("R3", 2, [P, D])
        gidx3 = ring("gidx3", 2, [P, 1], I32)
        sidx3 = ring("sidx3", 2, [P, 1], I32)
        dup3 = ring("dup3", 2, [P, 1])
        off3 = ring("off3", 2, [P, 1])
        al = ring("al", 4, [P, D])
        xs = ring("xs", 4, [P, C])
        sx = ring("sx", 2, [P, 3, C])
        sr = ring("sr", 2, [P, C])
        sp = ring("sp", 2, [P, C])
        spT = ring("spT", 2, [P, C])
        stat4 = ring("stat4", 2, [P, 6])
        mv4 = ring("mv4", 2, [P, 2])
        tiny4 = ring("tiny4", 2, [P, 8])
        y_out = ring("y_out", 2, [P, D])

        s_load = sem("s_load")
        s_loadw = sem("s_loadw")
        s_zero = sem("s_zero")
        s_zero0 = sem("s_zero0")
        s_zero1 = sem("s_zero1")
        s_iota = sem("s_iota")
        s_const = sem("s_const")
        s_deg_hot = sem("s_deg_hot")
        s_deg_mm = sem("s_deg_mm")
        s_sqrt = sem("s_sqrt")
        s_srow = [sem(f"s_srow{i}") for i in range(2)]
        s_low = sem("s_low")
        s_hotT = sem("s_hotT")
        s_look = sem("s_look")
        s_pick = sem("s_pick")
        s_wprep = sem("s_wprep")
        s_wT = sem("s_wT")
        s_wTc = sem("s_wTc")
        s_wmv = sem("s_wmv")
        e_trow = [sem(f"e_trow{i}") for i in range(2)]
        e_gidx = sem("e_gidx")
        e_gather = [sem(f"e_gather{i}") for i in range(4)]
        e_M = sem("e_M")
        e_idx = sem("e_idx")
        e_mm = sem("e_mm")
        e_ev = sem("e_ev")
        e_scat = [sem(f"e_scat{i}") for i in range(4)]
        n_sl = [sem(f"n_sl{i}") for i in range(2)]
        n_xl = [sem(f"n_xl{i}") for i in range(2)]
        n_z = sem("n_z")
        n_tr = sem("n_tr")
        n_zT = sem("n_zT")
        n_mm = sem("n_mm")
        n_res = sem("n_res")
        n_rs = sem("n_rs")
        n_rstd = sem("n_rstd")
        n_x1 = sem("n_x1")
        n_st = [sem(f"n_st{i}") for i in range(2)]
        f_trow = [sem(f"f_trow{i}") for i in range(2)]
        f_fT = [sem(f"f_fT{i}") for i in range(2)]
        f_gidx = sem("f_gidx")
        f_gather = [sem(f"f_gather{i}") for i in range(2)]
        f_proj = sem("f_proj")
        f_tr = sem("f_tr")
        f_hmm = sem("f_hmm")
        f_rawT = sem("f_rawT")
        f_soft = sem("f_soft")
        f_h = sem("f_h")
        f_wv = sem("f_wv")
        f_feat = sem("f_feat")
        f_m = sem("f_m")
        f_o = sem("f_o")
        f_us = sem("f_us")
        f_msg = sem("f_msg")
        f_M = sem("f_M")
        f_idx = sem("f_idx")
        f_mm = sem("f_mm")
        f_ev = sem("f_ev")
        f_scat = [sem(f"f_scat{i}") for i in range(2)]
        g_al = [sem(f"g_al{i}") for i in range(4)]
        g_xs = [sem(f"g_xs{i}") for i in range(4)]
        g_soft = sem("g_soft")
        g_sp = sem("g_sp")
        g_tr = sem("g_tr")
        g_spT = sem("g_spT")
        g_mm = sem("g_mm")
        g_res = sem("g_res")
        g_rs = sem("g_rs")
        g_rstd = sem("g_rstd")
        g_y = sem("g_y")
        g_st = [sem(f"g_st{i}") for i in range(2)]
        hold = {e: sem(f"hold_{e}") for e in ("pool", "sync", "vector")}

        def held(eng, s, value):
            if not isinstance(value, int) or value > 0:
                eng.wait_ge(s, value)
                eng.sem_inc(hold["pool" if eng is nc.gpsimd else "sync" if eng is nc.sync else "vector"], 1)

        K_M, K_IDX = 1, 3
        K_RES, K_RSTD = 5, 5
        K_PROJ, K_SOFT, K_PROD, K_MSG = 3, 4, 4, 3

        block = ctx.enter_context(nc.Block())

        @block.sync
        def _(sp_):
            for dst, src in ((src_i, src_cols), (dst_i, dst_cols), (ew, weight)):
                sp_.dma_start(dst[:, :], src).then_inc(s_load, 16)
            sp_.dma_start(rij[:, :, :], vec).then_inc(s_load, 16)

            def load_srow(g, u):
                held(sp_, s_low, g - 1)
                sp_.dma_start(srow[u][:, :], src_row[:, bass.ds(g * 512, 512)].broadcast_to([P, 512])) \
                   .then_inc(s_srow[u], 16)

            for g in range(2):
                load_srow(g, g)
            for dst, src in (
                (W0_s[:, :, :], W0.rearrange("(c p) n -> p c n", p=P)), (b0_s[:, :], b0.broadcast_to([P, D])),
                (Wins[:, :], Win_s), (Winv[:, :], Win_v), (Wf1_s[:, :], Wf1),
                (bf1_c[:, :], bf1), (Wf2_s[:, :], Wf2[:, 0:512]), (bf2_c[:, :], bf2),
                (W1s_r[:, :, :], W1_s.rearrange("(f k) c -> f k c", k=2)),
                (W1v_r[:, :, :], W1_v.rearrange("(f k) c -> f k c", k=2)),
                (W2s_r[:, :], W2_s), (W2v_r[:, :], W2_v),
            ):
                sp_.dma_start(dst, src).then_inc(s_loadw, 16)

            with sp_.Fori(1, T // 8) as j:
                for u in range(2):
                    load_srow(j * 2 + u, u)

            def load_trow(g, u):
                held(sp_, e_M, 2 * (g - 1))
                held(sp_, e_idx, 2 * K_IDX * (g - 1))
                sp_.dma_start(trow[u][:, :], dst_row[:, bass.ds(g * 256, 256)].broadcast_to([P, 256])) \
                   .then_inc(e_trow[u], 16)

            for g in range(2):
                load_trow(g, g)
            with sp_.Fori(1, T // 4) as j:
                for u in range(2):
                    load_trow(j * 2 + u, u)

            for u in range(4):
                sp_.wait_ge(e_scat[u], 16 * (T // 4))

            def nodes0(s, u):
                if live(s, 0):
                    held(sp_, n_z, s - 1)
                    sp_.dma_start(sl[u][:, :], rows(sum0, s)).then_inc(n_sl[u], 16)
                    held(sp_, n_res, K_RES * (s - 1))
                    sp_.dma_start(xl[u][:, :], rows(x, s)).then_inc(n_xl[u], 16)

            skewed(sp_, nodes0, 0, 4)

            def edges1(s, u):
                if live(s, 0):
                    held(sp_, f_hmm, s - 1)
                    sp_.dma_start(fT[u][:, :], rbf[:, bass.ds(s * P, P)]).then_inc(f_fT[u], 16)
                if live(s, 2):
                    t = s - 2
                    held(sp_, f_M, t - 1)
                    held(sp_, f_idx, K_IDX * (t - 1))
                    sp_.dma_start(trow3[u][:, :], src_row[:, bass.ds(t * P, P)].broadcast_to([P, P])) \
                       .then_inc(f_trow[u], 16)

            skewed(sp_, edges1, 2, 4)

            for u in range(2):
                sp_.wait_ge(f_scat[u], 16 * (T // 2))

            def nodes1(s, u):
                if live(s, 0):
                    held(sp_, g_y, s - 3)
                    sp_.dma_start(al[u][:, :], rows(sum1, s)).then_inc(g_al[u], 16)
                    held(sp_, g_res, 3 * (s - 3))
                    sp_.dma_start(xs[u][:, :], x1_d[bass.ds(s * P, P), 0:C]).then_inc(g_xs[u], 16)

            skewed(sp_, nodes1, 0, 4, 4)

        @block.gpsimd
        def _(pool):
            pool.iota(iota_i[:, :], [[1, 256]], base=0, channel_multiplier=0).then_inc(s_iota, 1)
            pool.iota(lane_i[:, :], [[P, 2]], base=0, channel_multiplier=1).then_inc(s_iota, 1)
            pool.iota(ident_i[:, :], [[1, P]], base=0, channel_multiplier=-1).then_inc(s_iota, 1)
            pool.iota(trash_i[:, :], [[0, T // 2], [P, 2]], base=NP, channel_multiplier=1).then_inc(s_iota, 1)

            def gather0(g, gp):
                for u in range(2):
                    k = 2 * gp + u
                    held(pool, e_gidx, 2 * g + u + 1)
                    held(pool, e_mm, g - 1)
                    pool.indirect_dma_start(G[k][:, :], None, x, bass.IndirectOffsetOnAxis(ap=gidx[k][:, :], axis=0)) \
                        .then_inc(e_gather[k], 16)

            def scatter0(g, gp, n):
                for u in range(2):
                    k = 2 * gp + u
                    held(pool, e_idx, K_IDX * (2 * g + u + 1))
                    held(pool, e_ev, 2 * g + u + 1)
                    if u == 0:
                        for v in range(2):
                            held(pool, e_scat[2 * (1 - gp) + v], 16 * (n + gp))
                    pool.indirect_dma_start(sum0, bass.IndirectOffsetOnAxis(ap=sidx[k][:, :], axis=0), R[k][:, :], None,
                                            compute_op=ALU.add).then_inc(e_scat[k], 16)

            gather0(0, 0)
            held(pool, s_zero0, 16 * 41)
            gather0(1, 1)
            scatter0(0, 0, 0)
            with pool.Fori(1, T // 4) as j:
                gather0(2 * j, 0)
                scatter0(2 * j - 1, 1, j - 1)
                gather0(2 * j + 1, 1)
                scatter0(2 * j, 0, j)
            scatter0(T // 2 - 1, 1, T // 4 - 1)

            for u in range(2):
                held(pool, n_st[u], 32 * (T // 2))
            held(pool, s_zero1, 16 * 22)

            def edges1(s, u):
                if live(s, 0):
                    held(pool, f_gidx, s + 1)
                    held(pool, f_tr, s - 1)
                    held(pool, f_proj, K_PROJ * (s - 1))
                    pool.indirect_dma_start(G3[u][:, :], None, x1_d, bass.IndirectOffsetOnAxis(ap=gidx3[u][:, :], axis=0)) \
                        .then_inc(f_gather[u], 16)
                if live(s, 4):
                    t = s - 4
                    held(pool, f_idx, K_IDX * (t + 1))
                    held(pool, f_ev, t + 1)
                    n = turn(t, u, 2) + u
                    held(pool, f_scat[1 - u], 16 * n)
                    pool.indirect_dma_start(sum1, bass.IndirectOffsetOnAxis(ap=sidx3[u][:, :], axis=0), R3[u][:, :], None,
                                            compute_op=ALU.add).then_inc(f_scat[u], 16)

            skewed(pool, edges1, 4, 6)

        @block.scalar
        def _(act):
            act.wait_ge(s_zero, 1)
            with act.Fori(0, 41) as j:
                act.dma_start(sum0[bass.ds(j * 256, 256), :].rearrange("(p r) d -> p (r d)", r=2), zeros[:, :]) \
                   .then_inc(s_zero0, 16)
            act.wait_ge(s_const, 11)
            act.activation(degs[:, :], degm[:, :], ACT.Sqrt).then_inc(s_sqrt, 1)
            act.activation(rn[:, :], rsq[:, :, 0], ACT.Sqrt).then_inc(s_sqrt, 1)
            with act.Fori(0, 20) as j:
                act.dma_start(sum1[bass.ds(j * 512, 512), 0:C].rearrange("(p r) d -> p r d", r=4),
                              zeros[:, 0:512].rearrange("p (r d) -> p r d", r=4)).then_inc(s_zero1, 16)
            for q in range(2):
                act.dma_start(sum1[NP + q * P:NP + (q + 1) * P, :], zeros[:, 0:D]).then_inc(s_zero1, 16)

            act.wait_ge(s_wT, 1)
            act.copy(W1vT[:, :, :], bank[7][:, 0:256].rearrange("p (k c) -> p k c", k=2)).then_inc(s_wTc, 1)
            act.wait_ge(s_wmv, 1)
            act.mul(MV[:, 0, :], bank[7][:, 256:384], 1.0 / (16.0 * C)).then_inc(s_wTc, 1)
            act.mul(MV[:, 1, :], bank[7][:, 384:512], Y0 / (16.0 * C)).then_inc(s_wTc, 1)

            def evac0(g, gp, n):
                for u in range(2):
                    k = 2 * gp + u
                    act.wait_ge(e_mm, g + 1)
                    wait(act, e_scat[k], 16 * n)
                    act.copy(R[k][:, :], bank[k][:, :]).then_inc(e_ev, 1)

            for g in range(2):
                evac0(g, g, 0)
            with act.Fori(1, T // 4) as j:
                for gp in range(2):
                    evac0(2 * j + gp, gp, j)

            def nodes0(s, u):
                if live(s, 0):
                    act.wait_ge(n_tr, s + 1)
                    wait(act, n_mm, s - 1)
                    act.copy(zT[u][:, :], bank[u][:, :]).then_inc(n_zT, 1)
                if live(s, 1):
                    v = 1 - u
                    act.wait_ge(n_res, K_RES * s)
                    act.activation(tiny[v][:, 1:2], tiny[v][:, 0:1], ACT.Ln).then_inc(n_rs, 1)
                    act.wait_ge(n_rs, 2 * s - 1)
                    act.activation(tiny[v][:, 2:3], tiny[v][:, 1:2], ACT.Exp, scale=-0.5).then_inc(n_rs, 1)
                if live(s, 2):
                    act.wait_ge(n_rstd, K_RSTD * (s - 1))
                    n = turn(s - 2, u, 2)
                    wait(act, n_st[u], 32 * n)
                    act.activation(x1[u][:, :], res[u][:, :], ACT.Identity, bias=tiny[u][:, 6:7], scale=tiny[u][:, 5:6]) \
                       .then_inc(n_x1, 1)
                    act.wait_ge(n_x1, s - 1)
                    act.dma_start(rows(x1_d, s - 2), x1[u][:, :]).then_inc(n_st[u], 16)
                    act.dma_start(sum1[bass.ds((s - 2) * P, P), C:D], x1[u][:, C:D]).then_inc(n_st[u], 16)

            skewed(act, nodes0, 2, 4)

            def edges1(s, u):
                if live(s, 0):
                    act.wait_ge(f_tr, s + 1)
                    wait(act, f_wv, s - 1)
                    act.copy(rawT[u][:, 0:512], bank[0][:, :]).then_inc(f_rawT, 1)
                    act.wait_ge(f_hmm, s + 1)
                    act.copy(rawT[u][:, 512:640], bank[1][:, 0:P]).then_inc(f_rawT, 1)
                    wait(act, f_h, s - 1)
                    st = Stage(f_soft, s, K_SOFT)
                    st.mark(act.activation(hr[u][:, :], bank[1][:, P:2 * P], ACT.Relu, bias=bf1_c[:, :]))
                    st.mark(act.activation(hx[u][:, 0, :], bank[1][:, P:2 * P], ACT.Abs, bias=bf1_c[:, :]))
                    st.settle(act)
                    st.mark(act.activation(hx[u][:, 1, :], hx[u][:, 0, :], ACT.Exp, scale=-1.0))
                    st.settle(act)
                    st.mark(act.activation(hx[u][:, 2, :], hx[u][:, 1, :], ACT.Ln, bias=1.0))
                if live(s, 1):
                    t, v = s - 1, 1 - u
                    act.wait_ge(f_wv, t + 1)
                    wait(act, f_m, K_PROD * (t - 1))
                    act.copy(feat[v][:, 0:512], bank[2][:, :]).then_inc(f_feat, 1)
                    act.copy(feat[v][:, 512:640], bank[3][:, 0:P]).then_inc(f_feat, 1)
                if live(s, 2):
                    t = s - 2
                    act.wait_ge(f_o, t + 1)
                    wait(act, f_mm, t - 1)
                    act.copy(msg[u][:, 0:256], bank[5][:, 0:256]).then_inc(f_us, 1)
                if live(s, 3):
                    t, v = s - 3, 1 - u
                    act.wait_ge(f_mm, t + 1)
                    n = turn(t, v, 2)
                    wait(act, f_scat[v], 16 * n)
                    act.copy(R3[v][:, :], bank[7][:, :]).then_inc(f_ev, 1)

            skewed(act, edges1, 3, 6)

            def nodes1(s, a):
                if live(s, 0):
                    u = a % 2
                    act.wait_ge(g_al[a], 16 * (turn(s, a, 4) + 1))
                    wait(act, g_sp, 2 * (s - 1))
                    st = Stage(g_soft, s, 3)
                    st.mark(act.activation(sx[u][:, 0, :], al[a][:, 0:C], ACT.Abs))
                    st.settle(act)
                    st.mark(act.activation(sx[u][:, 1, :], sx[u][:, 0, :], ACT.Exp, scale=-1.0))
                    st.settle(act)
                    st.mark(act.activation(sx[u][:, 2, :], sx[u][:, 1, :], ACT.Ln, bias=1.0))
                if live(s, 1):
                    t, v = s - 1, (a - 1) % 2
                    act.wait_ge(g_tr, t + 1)
                    wait(act, g_mm, t - 1)
                    act.copy(spT[v][:, :], bank[v][:, 0:P]).then_inc(g_spT, 1)
                if live(s, 2):
                    t, u = s - 2, a % 2
                    act.wait_ge(g_rstd, (K_RSTD + 1) * t + 1)
                    act.activation(tiny4[u][:, 1:2], tiny4[u][:, 0:1], ACT.Ln).then_inc(g_rs, 1)
                    act.wait_ge(g_rs, 2 * t + 1)
                    act.activation(tiny4[u][:, 2:3], tiny4[u][:, 1:2], ACT.Exp, scale=-0.5).then_inc(g_rs, 1)
                if live(s, 3):
                    t, b, v = s - 3, (a - 3) % 4, (a - 3) % 2
                    act.wait_ge(g_rstd, (K_RSTD + 1) * (t + 1))
                    wait(act, g_st[v], 16 * turn(t, v, 2))
                    act.activation(y_out[v][:, :], al[b][:, :], ACT.Identity, bias=tiny4[v][:, 6:7],
                                   scale=tiny4[v][:, 5:6]).then_inc(g_y, 1)
                    act.wait_ge(g_y, t + 1)
                    act.dma_start(rows(out, t), y_out[v][:, :]).then_inc(g_st[v], 16)

            skewed(act, nodes1, 3, 8, 4)
            for v in range(2):
                act.wait_ge(g_st[v], 16 * (T // 2))

        @block.vector
        def _(dve):
            count = [0]

            def link(ins):
                count[0] += 1
                ins.then_inc(s_const, 1)
                dve.wait_ge(s_const, count[0])

            dve.memset(zeros[:, :], 0.0).then_inc(s_zero, 1)
            dve.wait_ge(s_iota, 4)
            dve.tensor_copy(iota_f[:, :], iota_i[:, :])
            dve.tensor_copy(lane[:, :], lane_i[:, :])
            dve.tensor_copy(trash[:, :], trash_i[:, :])
            dve.wait_ge(s_load, 64)
            dve.tensor_copy(src_f[:, :], src_i[:, :])
            dve.tensor_copy(dst_f[:, :], dst_i[:, :])
            dve.tensor_scalar(part_i[:, 0, :], dst_i[:, :], 127, None, ALU.bitwise_and)
            dve.tensor_scalar(part_i[:, 1, :], dst_i[:, :], 7, None, ALU.logical_shift_right)
            dve.tensor_scalar(part_i[:, 2, :], src_i[:, :], 127, None, ALU.bitwise_and)
            dve.tensor_scalar(part_i[:, 3, :], src_i[:, :], 7, None, ALU.logical_shift_right)
            link(dve.tensor_scalar(ident[:, :], ident_i[:, :], 0.0, None, ALU.is_equal))
            dve.tensor_tensor(to_trash_src[:, :], trash[:, :], src_f[:, :], ALU.subtract)
            dve.tensor_tensor(to_trash_dst[:, :], trash[:, :], dst_f[:, :], ALU.subtract)
            for u in range(2):
                dve.tensor_scalar(before[:, u, :], iota_f[:, :], lane[:, u:u + 1], None, ALU.is_lt)
            link(dve.tensor_copy(part[:, :, :], part_i[:, :, :]))

            def hots(t, u):
                wait(dve, s_deg_mm, t)
                dve.tensor_scalar(hot_lo[u][:, :], iota_f[:, 0:P], part[:, 0, bass.ds(t, 1)], None, ALU.is_equal) \
                   .then_inc(s_deg_hot, 1)
                dve.tensor_scalar(hot_hi[u][:, :], iota_f[:, 0:T], part[:, 1, bass.ds(t, 1)], ew[:, bass.ds(t, 1)],
                                  ALU.is_equal, ALU.mult).then_inc(s_deg_hot, 1)

            for t in range(2):
                hots(t, t)
            with dve.Fori(1, T // 2) as j:
                for u in range(2):
                    hots(2 * j + u, u)

            dve.tensor_tensor(rsq[:, :, :], rij[:, :, :], rij[:, :, :], ALU.mult)
            dve.wait_ge(s_deg_mm, T + 1)
            link(dve.tensor_scalar(deg[:, :], bank[6][:, 0:T], 1.0, None, ALU.add))
            link(dve.tensor_scalar(degm[:, :], deg[:, :], 1e-34, None, ALU.max))
            link(dve.tensor_scalar(deg[:, :], deg[:, :], 0.0, None, ALU.is_gt))
            link(dve.tensor_tensor(rsq[:, :, 0], rsq[:, :, 0], rsq[:, :, 1], ALU.add))
            link(dve.tensor_tensor(rsq[:, :, 0], rsq[:, :, 0], rsq[:, :, 2], ALU.add))
            for q in range(2):
                k = Y0 / (16.0 * C ** 0.5) if q == 0 else 1.0 / (16.0 * C ** 0.5 * 3.0 ** 0.5)
                dve.wait_ge(s_loadw, 16 * 12)
                link(dve.tensor_scalar(W1s_s[:, q, :], W1s_r[:, q, :], k, None, ALU.mult))
            link(dve.tensor_scalar(W2s_s[:, :], W2s_r[:, :], 1.0 / C ** 0.5, None, ALU.mult))
            link(dve.tensor_copy(degt[:, :], degm[:, :]))
            dve.wait_ge(s_sqrt, 2)
            link(dve.reciprocal(dis[:, :], degs[:, :]))
            link(dve.reciprocal(rn[:, :], rn[:, :]))
            link(dve.tensor_tensor(degt[:, :], degt[:, :], dis[:, :], ALU.mult))
            link(dve.tensor_tensor(degt[:, :], degt[:, :], dis[:, :], ALU.mult))
            link(dve.tensor_scalar(degt[:, :], degt[:, :], -0.5, 1.5, ALU.mult, ALU.add))
            link(dve.tensor_tensor(dis[:, :], dis[:, :], degt[:, :], ALU.mult))
            link(dve.tensor_tensor(dis[:, :], dis[:, :], deg[:, :], ALU.mult))
            link(dve.scalar_tensor_tensor(Y[:, :, :], rij[:, :, :], Y1, rn[:, :].unsqueeze(2).broadcast_to([P, T, 3]),
                                          ALU.mult, ALU.mult))
            dve.sem_inc(s_pick, 1)

            def transposed_hots(g, u, n):
                dve.wait_ge(s_srow[u], 16 * (n + 1))
                wait(dve, s_hotT, g - 1)
                dve.tensor_scalar(slow[u][:, :], srow[u][:, :], 127, None, ALU.bitwise_and).then_inc(s_low, 1)
                dve.wait_ge(s_low, g + 1)
                wait(dve, s_look, g - 1)
                dve.tensor_scalar(hotT[u][:, :], slow[u][:, :], lane[:, 0:1], None, ALU.is_equal).then_inc(s_hotT, 1)

            def pick(g, u):
                dve.wait_ge(s_look, g + 1)
                for q in range(4):
                    t = 4 * g + q
                    ins = dve.scalar_tensor_tensor(junk80[:, 4 * u + q, :], iota_f[:, 0:T], part[:, 3, bass.ds(t, 1)],
                                                   bank[u][:, q * T:(q + 1) * T], ALU.is_equal, ALU.mult,
                                                   accum_out=dsrc[:, bass.ds(t, 1)])
                ins.then_inc(s_pick, 1)

            transposed_hots(0, 0, 0)
            transposed_hots(1, 1, 0)
            pick(0, 0)
            with dve.Fori(1, T // 8) as j:
                transposed_hots(2 * j, 0, j)
                pick(2 * j - 1, 1)
                transposed_hots(2 * j + 1, 1, j)
                pick(2 * j, 0)
            pick(T // 4 - 1, 1)
            dve.wait_ge(s_pick, T // 4 + 1)
            link(dve.tensor_tensor(coef[:, :], ew[:, :], dsrc[:, :], ALU.mult))

            def combine0(g, gp, n):
                for u in range(2):
                    k = 2 * gp + u
                    wait(dve, e_gather[k], 16 * n)
                    dve.tensor_scalar(gidx[k][:, :], src_i[:, bass.ds(2 * g + u, 1)], 0.0, None, ALU.add).then_inc(e_gidx, 1)
                dve.wait_ge(e_trow[gp], 16 * (n + 1))
                for u in range(2):
                    k, t = 2 * gp + u, 2 * g + u
                    wait(dve, e_mm, g - 1)
                    dve.tensor_scalar(M[k][:, :], trow[gp][:, :], dst_f[:, bass.ds(t, 1)], coef[:, bass.ds(t, 1)],
                                      ALU.is_equal, ALU.mult).then_inc(e_M, 1)
                for u in range(2):
                    k, t = 2 * gp + u, 2 * g + u
                    st = Stage(e_idx, t, K_IDX)
                    st.mark(dve.scalar_tensor_tensor(junk[k][:, :], trow[gp][:, :], dst_f[:, bass.ds(t, 1)], before[:, u, :],
                                                     ALU.is_equal, ALU.mult, accum_out=dup[k][:, :]))
                    st.settle(dve)
                    st.mark(dve.tensor_scalar(off[k][:, :], dup[k][:, :], 1.0, to_trash_dst[:, bass.ds(t, 1)], ALU.min, ALU.mult))
                    st.settle(dve)
                    wait(dve, e_scat[k], 16 * n)
                    st.mark(dve.tensor_scalar(sidx[k][:, :], off[k][:, :], dst_f[:, bass.ds(t, 1)], None, ALU.add))

            for g in range(2):
                combine0(g, g, 0)
            with dve.Fori(1, T // 4) as j:
                for gp in range(2):
                    combine0(2 * j + gp, gp, j)

            def residual0(t, v):
                st = Stage(n_res, t, K_RES)
                dve.wait_ge(n_mm, t + 1)
                st.mark(dve.scalar_tensor_tensor(pre[v][:, :], bank[2 + v][:, :], dis[:, bass.ds(t, 1)], b0_s[:, :],
                                                 ALU.mult, ALU.add))
                st.settle(dve)
                wait(dve, n_x1, t - 1)
                st.mark(dve.scalar_tensor_tensor(res[v][:, :], pre[v][:, :], 0.0, xl[v][:, :], ALU.max, ALU.add))
                st.settle(dve)
                st.mark(dve.bn_stats(stat[v][:, :], res[v][:, :]))
                held(dve, n_res, st.reached())
                st.mark(dve.bn_aggr(mv[v][:, :], stat[v][:, :]))
                st.settle(dve)
                st.mark(dve.tensor_scalar(tiny[v][:, 0:1], mv[v][:, 1:2], EPS, None, ALU.add))

            def rstd(st, w, mvar):
                st.mark(dve.tensor_scalar(w[:, 3:4], w[:, 2:3], w[:, 2:3], w[:, 0:1], ALU.mult, ALU.mult))
                st.settle(dve)
                st.mark(dve.tensor_scalar(w[:, 4:5], w[:, 3:4], -0.5, 1.5, ALU.mult, ALU.add))
                st.settle(dve)
                st.mark(dve.tensor_tensor(w[:, 5:6], w[:, 4:5], w[:, 2:3], ALU.mult))
                st.settle(dve)
                st.mark(dve.tensor_scalar(w[:, 6:7], mvar[:, 0:1], w[:, 5:6], -1.0, ALU.mult, ALU.mult))

            def nodes0(s, u):
                if live(s, 0):
                    n = turn(s, u, 2)
                    dve.wait_ge(n_sl[u], 16 * (n + 1))
                    dve.wait_ge(n_xl[u], 16 * (n + 1))
                    wait(dve, n_tr, s - 1)
                    dve.scalar_tensor_tensor(zl[u][:, :], xl[u][:, :], dis[:, bass.ds(s, 1)], sl[u][:, :],
                                             ALU.mult, ALU.add).then_inc(n_z, 1)
                if live(s, 1):
                    residual0(s - 1, 1 - u)
                    dve.wait_ge(n_rs, 2 * s)
                    st = Stage(n_rstd, s - 1, K_RSTD)
                    rstd(st, tiny[1 - u], mv[1 - u])
                    st.settle(dve)
                    dve.sem_inc(n_rstd, 1)

            skewed(dve, nodes0, 1, 4)

            def edges1(s, u):
                if live(s, 0):
                    n = turn(s, u, 2)
                    wait(dve, f_gather[u], 16 * n)
                    dve.tensor_scalar(gidx3[u][:, :], dst_i[:, bass.ds(s, 1)], 0.0, None, ALU.add).then_inc(f_gidx, 1)
                    dve.wait_ge(f_gather[u], 16 * (n + 1))
                    gv = G3[u][:, C:D].rearrange("p (c i) -> p c i", i=3)
                    wait(dve, f_tr, s - 1)
                    st = Stage(f_proj, s, K_PROJ)
                    st.mark(dve.tensor_scalar(proj[u][:, :], gv[:, :, 0], Y[:, bass.ds(s, 1), 0], None, ALU.mult))
                    for i in (1, 2):
                        st.settle(dve)
                        st.mark(dve.scalar_tensor_tensor(proj[u][:, :], gv[:, :, i], Y[:, bass.ds(s, 1), i], proj[u][:, :],
                                                         ALU.mult, ALU.add))
                    wait(dve, f_wv, s - 1)
                    dve.wait_ge(f_soft, K_SOFT * (s + 1))
                    dve.scalar_tensor_tensor(h[u][:, :], hx[u][:, 2, :], -LOG2, hr[u][:, :], ALU.add, ALU.add).then_inc(f_h, 1)
                if live(s, 1):
                    t, v = s - 1, 1 - u
                    dve.wait_ge(f_wv, t + 1)
                    dve.wait_ge(f_feat, 2 * (t + 1))
                    wait(dve, f_o, t - 1)
                    st = Stage(f_m, t, K_PROD)
                    f_s, f_z = feat[v][:, 512:640], feat[v][:, 384:512]
                    for q, fe in ((0, f_s), (1, f_z), (2, f_s)):
                        st.mark(dve.scalar_tensor_tensor(m[v][:, q * P:(q + 1) * P], bank[4][:, q * P:(q + 1) * P],
                                                         bf2_c[:, q:q + 1], fe, ALU.add, ALU.mult))
                    st.mark(dve.scalar_tensor_tensor(
                        m[v][:, 384:768].rearrange("p (i e) -> p i e", i=3),
                        bank[4][:, 384:512].unsqueeze(1).broadcast_to([P, 3, P]), bf2_c[:, 3:4],
                        feat[v][:, 0:384].rearrange("p (i e) -> p i e", i=3), ALU.add, ALU.mult))
                if live(s, 2):
                    t = s - 2
                    dve.wait_ge(f_us, t + 1)
                    dve.wait_ge(f_o, t + 1)
                    st = Stage(f_msg, t, K_MSG)
                    mo = msg[u][:, 256:640].rearrange("p (c i) -> p c i", i=3)
                    for i in range(3):
                        st.mark(dve.scalar_tensor_tensor(mo[:, :, i], msg[u][:, 0:P], Y[:, bass.ds(t, 1), i],
                                                         bank[6][:, i * P:(i + 1) * P], ALU.mult, ALU.add))

                if live(s, 3):
                    t, v = s - 3, 1 - u
                    n = turn(t, v, 2)
                    dve.wait_ge(f_trow[v], 16 * (n + 1))
                    wait(dve, f_mm, t - 1)
                    dve.tensor_scalar(M3[v][:, :], trow3[v][:, :], src_f[:, bass.ds(t, 1)], ew[:, bass.ds(t, 1)],
                                      ALU.is_equal, ALU.mult).then_inc(f_M, 1)
                    si = Stage(f_idx, t, K_IDX)
                    si.mark(dve.scalar_tensor_tensor(junk[v][:, 0:P], trow3[v][:, :], src_f[:, bass.ds(t, 1)], before[:, 0, 0:P],
                                                     ALU.is_equal, ALU.mult, accum_out=dup3[v][:, :]))
                    si.settle(dve)
                    si.mark(dve.tensor_scalar(off3[v][:, :], dup3[v][:, :], 1.0, to_trash_src[:, bass.ds(t, 1)], ALU.min, ALU.mult))
                    si.settle(dve)
                    wait(dve, f_scat[v], 16 * n)
                    si.mark(dve.tensor_scalar(sidx3[v][:, :], off3[v][:, :], src_f[:, bass.ds(t, 1)], None, ALU.add))

            skewed(dve, edges1, 3, 6)

            def nodes1(s, a):
                if live(s, 0):
                    u = a % 2
                    dve.wait_ge(g_al[a], 16 * (turn(s, a, 4) + 1))
                    wait(dve, g_tr, s - 1)
                    st = Stage(g_sp, s, 2)
                    st.mark(dve.tensor_scalar(sr[u][:, :], al[a][:, 0:C], 0.0, -LOG2, ALU.max, ALU.add))
                    st.settle(dve)
                    dve.wait_ge(g_soft, 3 * (s + 1))
                    st.mark(dve.tensor_tensor(sp[u][:, :], sr[u][:, :], sx[u][:, 2, :], ALU.add))
                if live(s, 1):
                    t, a, v = s - 1, (a - 1) % 4, (a - 1) % 2
                    dve.wait_ge(g_mm, t + 1)
                    dve.wait_ge(g_xs[a], 16 * (turn(t, a, 4) + 1))
                    st = Stage(g_res, t, 3)
                    st.mark(dve.tensor_tensor(al[a][:, 0:C], bank[2 + v][:, 0:C], xs[a][:, :], ALU.add))
                    st.settle(dve)
                    st.mark(dve.bn_stats(stat4[v][:, :], al[a][:, :]))
                    held(dve, g_res, st.reached())
                    held(dve, g_y, t - 1)
                    st.mark(dve.bn_aggr(mv4[v][:, :], stat4[v][:, :]))
                    st.settle(dve)
                    sv = Stage(g_rstd, t, K_RSTD + 1)
                    sv.mark(dve.tensor_scalar(tiny4[v][:, 0:1], mv4[v][:, 1:2], EPS, None, ALU.add))
                    dve.wait_ge(g_rs, 2 * (t + 1))
                    rstd(sv, tiny4[v], mv4[v])
                    sv.settle(dve)
                    dve.sem_inc(g_rstd, 1)

            skewed(dve, nodes1, 1, 4, 4)

        @block.tensor
        def _(pe):
            pe.wait_ge(s_zero, 1)
            pe.matmul(bank[6][:, 0:T], zeros[:, 0:P], zeros[:, 0:T], start=True, stop=False,
                      skip_group_check=True).then_inc(s_deg_mm, 1)

            def deg_mm(t, u):
                pe.wait_ge(s_deg_hot, 2 * t + 2)
                pe.matmul(bank[6][:, 0:T], hot_lo[u][:, :], hot_hi[u][:, :], start=False, stop=False,
                          skip_group_check=True).then_inc(s_deg_mm, 1)

            with pe.Fori(0, T // 2) as j:
                for u in range(2):
                    deg_mm(2 * j + u, u)

            def look(g, u):
                pe.wait_ge(s_hotT, g + 1)
                pe.wait_ge(s_pick, g if not isinstance(g, int) else max(g, 1))
                for q in range(4):
                    ins = pe.matmul(bank[u][:, q * T:(q + 1) * T], hotT[u][:, q * P:(q + 1) * P], dis[:, :],
                                    start=True, stop=True)
                ins.then_inc(s_look, 1)

            for g in range(2):
                look(g, g)
            with pe.Fori(1, T // 8) as j:
                for u in range(2):
                    look(2 * j + u, u)

            pe.wait_ge(s_loadw, 16 * 12)
            pe.wait_ge(s_const, 2)
            for q in range(2):
                ins = pe.transpose(bank[7][:, q * P:(q + 1) * P], W1v_r[:, q, :], ident[:, :])
            ins.then_inc(s_wT, 1)
            pe.wait_ge(s_wTc, 1)
            for q in range(2):
                ins = pe.matmul(bank[7][:, 256 + q * P:256 + (q + 1) * P], W1vT[:, q, :], W2v_r[:, :], start=True, stop=True)
            ins.then_inc(s_wmv, 1)

            def sums0(g, gp, n):
                for u in range(2):
                    pe.wait_ge(e_gather[2 * gp + u], 16 * (n + 1))
                pe.wait_ge(e_M, 2 * g + 2)
                wait(pe, e_ev, 2 * (g - 1))
                for u in range(2):
                    for v in range(2):
                        ins = pe.matmul(bank[2 * gp + u][:, :], M[2 * gp + v][:, u * P:(u + 1) * P], G[2 * gp + v][:, :],
                                        start=(v == 0), stop=(v == 1))
                ins.then_inc(e_mm, 1)

            pe.wait_ge(s_pick, T // 4 + 1)
            for g in range(2):
                sums0(g, g, 0)
            with pe.Fori(1, T // 4) as j:
                for gp in range(2):
                    sums0(2 * j + gp, gp, j)

            pe.wait_ge(e_ev, T)
            pe.wait_ge(s_loadw, 16 * 12)

            def nodes0(s, u):
                if live(s, 0):
                    pe.wait_ge(n_z, s + 1)
                    wait(pe, n_zT, s - 1)
                    for c in range(4):
                        ins = pe.transpose(bank[u][:, c * P:(c + 1) * P], zl[u][:, c * P:(c + 1) * P], ident[:, :])
                    ins.then_inc(n_tr, 1)
                if live(s, 1):
                    t, v = s - 1, 1 - u
                    pe.wait_ge(n_zT, t + 1)
                    wait(pe, n_res, K_RES * (t - 1))
                    for c in range(4):
                        ins = pe.matmul(bank[2 + v][:, :], zT[v][:, c * P:(c + 1) * P], W0_s[:, c, :],
                                        start=(c == 0), stop=(c == 3))
                    ins.then_inc(n_mm, 1)

            skewed(pe, nodes0, 1, 4)

            pe.wait_ge(n_zT, T)
            pe.wait_ge(n_res, K_RES * T)
            pe.wait_ge(s_wTc, 3)
            pe.wait_ge(s_const, 11)

            def edges1(s, u):
                if live(s, 0):
                    n = turn(s, u, 2)
                    pe.wait_ge(f_gather[u], 16 * (n + 1))
                    pe.wait_ge(f_proj, K_PROJ * (s + 1))
                    wait(pe, f_rawT, 2 * s)
                    wait(pe, f_soft, K_SOFT * s)
                    gv = G3[u][:, C:D].rearrange("p (c i) -> p c i", i=3)
                    for i in range(3):
                        pe.transpose(bank[0][:, i * P:(i + 1) * P], gv[:, :, i], ident[:, :])
                    pe.transpose(bank[0][:, 384:512], proj[u][:, :], ident[:, :])
                    pe.transpose(bank[1][:, 0:P], G3[u][:, 0:C], ident[:, :]).then_inc(f_tr, 1)
                    pe.wait_ge(f_fT[u], 16 * (n + 1))
                    pe.matmul(bank[1][:, P:2 * P], Wf1_s[:, :], fT[u][:, :], start=True, stop=True).then_inc(f_hmm, 1)
                if live(s, 1):
                    t, v = s - 1, 1 - u
                    pe.wait_ge(f_rawT, 2 * (t + 1))
                    wait(pe, f_feat, 2 * t)
                    pe.matmul(bank[2][:, :], Winv[:, :], rawT[v][:, 0:512], start=True, stop=True)
                    pe.matmul(bank[3][:, 0:P], Wins[:, :], rawT[v][:, 512:640], start=True, stop=True)
                    pe.wait_ge(f_h, t + 1)
                    wait(pe, f_m, K_PROD * t)
                    for q in range(4):
                        base = 256 * (q // 2) + q % 2
                        ins = pe.matmul(bank[4][:, q * P:(q + 1) * P], Wf2_s[:, base:base + 255:2], h[v][:, :],
                                        start=True, stop=True)
                    ins.then_inc(f_wv, 1)
                if live(s, 2):
                    t = s - 2
                    pe.wait_ge(f_m, K_PROD * (t + 1))
                    wait(pe, f_us, t)
                    wait(pe, f_msg, K_MSG * t)
                    pe.matmul(bank[5][:, 0:P], m[u][:, 256:384], MV[:, 0, :], start=True, stop=True)
                    for q in range(2):
                        pe.matmul(bank[5][:, P:2 * P], m[u][:, q * P:(q + 1) * P], W1s_s[:, q, :], start=(q == 0), stop=(q == 1))
                    for i in range(3):
                        ins = pe.matmul(bank[6][:, i * P:(i + 1) * P], m[u][:, (3 + i) * P:(4 + i) * P], MV[:, 1, :],
                                        start=True, stop=True)
                    ins.then_inc(f_o, 1)
                if live(s, 3):
                    t, v = s - 3, 1 - u
                    pe.wait_ge(f_msg, K_MSG * (t + 1))
                    pe.wait_ge(f_us, t + 1)
                    pe.wait_ge(f_M, t + 1)
                    wait(pe, f_ev, t)
                    pe.matmul(bank[7][:, :], M3[v][:, :], msg[v][:, P:640], start=True, stop=True).then_inc(f_mm, 1)

            skewed(pe, edges1, 3, 6)

            pe.wait_ge(f_ev, T)

            def nodes1(s, u):
                if live(s, 0):
                    pe.wait_ge(g_sp, 2 * (s + 1))
                    wait(pe, g_spT, s - 1)
                    pe.transpose(bank[u][:, 0:P], sp[u][:, :], ident[:, :]).then_inc(g_tr, 1)
                if live(s, 1):
                    t, v = s - 1, 1 - u
                    pe.wait_ge(g_spT, t + 1)
                    wait(pe, g_res, 3 * (t - 1))
                    pe.matmul(bank[2 + v][:, 0:C], spT[v][:, :], W2s_s[:, :], start=True, stop=True).then_inc(g_mm, 1)

            skewed(pe, nodes1, 1, 4)


def kernel(x, src, dst, edge_attr_20, edge_attr_3, edge_weight, L0_gnn_W, L0_gnn_b, L1_gnn_W_in2f_s, L1_gnn_W_in2f_v,
           L1_gnn_Wf1, L1_gnn_bf1, L1_gnn_Wf2, L1_gnn_bf2, L1_gnn_W1_s, L1_gnn_W1_v, L1_gnn_W2_s, L1_gnn_W2_v):
    import concourse.bacc as bacc
    from concourse.bass_utils import run_bass_kernel_spmd

    def padded(a, value=0):
        a = np.asarray(a)
        out = np.full((NP,) + a.shape[1:], value, a.dtype)
        out[:N] = a
        return out

    def columns(a):
        return np.ascontiguousarray(np.moveaxis(a.reshape((T, P) + a.shape[1:]), 0, 1))

    ends = []
    for a in (src, dst):
        a = padded(a)
        a[N:] = np.arange(N, NP, dtype=a.dtype)
        ends.append(a)
    s, d = ends
    bf2 = np.asarray(L1_gnn_bf2)[:512].reshape(2, C, 2)
    arrays = {
        "x": padded(x),
        "src_cols": columns(s), "dst_cols": columns(d), "src_row": s.reshape(1, NP), "dst_row": d.reshape(1, NP),
        "weight": columns(padded(edge_weight)),
        "rbf": np.ascontiguousarray(padded(edge_attr_20).T),
        "vec": columns(padded(edge_attr_3, 1)),
        "W0": np.asarray(L0_gnn_W), "b0": np.asarray(L0_gnn_b).reshape(1, D),
        "Win_s": np.asarray(L1_gnn_W_in2f_s), "Win_v": np.asarray(L1_gnn_W_in2f_v),
        "Wf1": np.asarray(L1_gnn_Wf1), "bf1": np.asarray(L1_gnn_bf1).reshape(C, 1),
        "Wf2": np.asarray(L1_gnn_Wf2), "bf2": np.ascontiguousarray(bf2.transpose(1, 0, 2).reshape(C, 4)),
        "W1_s": np.asarray(L1_gnn_W1_s), "W1_v": np.asarray(L1_gnn_W1_v),
        "W2_s": np.asarray(L1_gnn_W2_s), "W2_v": np.asarray(L1_gnn_W2_v),
    }
    nc = bacc.Bacc("TRN2", target_bir_lowering=False, num_devices=1)
    args = [nc.dram_tensor(n, a.shape, mybir.dt.from_np(a.dtype), kind="ExternalInput").ap() for n, a in arrays.items()]
    args.append(nc.dram_tensor("out", (NP, D), F32, kind="ExternalOutput").ap())
    build(nc, *args)
    r = run_bass_kernel_spmd(nc, [arrays], core_ids=[0])
    return r.results[0]["out"][:N]
```

```python
from contextlib import ExitStack

import numpy as np

import concourse.bass as bass
from concourse import mybir

F32 = mybir.dt.float32
I32 = mybir.dt.int32
ALU = mybir.AluOpType
ACT = mybir.ActivationFunctionType

P = 128
N = 10000
T = 80
NP = T * P
D = 512
C = 128
RBF = 20
T2 = T // 2
TRASH = 2 * P
EPS = 1e-5
LOG2 = float(np.log(2.0))
Y0 = float(1.0 / np.sqrt(4.0 * np.pi))
Y1 = float(np.sqrt(3.0 / (4.0 * np.pi)))


def skewed(eng, step, tail, lead, unroll=4, steps=T):
    for s in range(lead):
        step(s, s % unroll)
    with eng.Fori(lead // unroll, steps // unroll) as j:
        for u in range(unroll):
            step(j * unroll + u, u)
    for s in range(steps, steps + tail):
        step(s, s % unroll)


def live(s, lag, steps=T):
    return not isinstance(s, int) or 0 <= s - lag < steps


def turn(t, slot, n):
    return t // n if isinstance(t, int) else (t - slot) // n


def wait(eng, sem, value):
    if not isinstance(value, int) or value > 0:
        eng.wait_ge(sem, value)


class Stage:

    def __init__(self, sem, t, total):
        self.sem, self.t, self.total, self.n = sem, t, total, 0

    def mark(self, ins):
        self.n += 1
        ins.then_inc(self.sem, 1)

    def reached(self):
        return self.t * self.total + self.n

    def settle(self, eng):
        eng.wait_ge(self.sem, self.reached())


def rows(dram, t):
    return dram[bass.ds(t * P, P), :]


def pair_rows(dram, s, c0, c1):
    return dram[bass.ds(s * 2 * P, 2 * P), c0:c1].rearrange("(k p) d -> p k d", p=P)


def build(nc, x, src_cols, dst_cols, src_row, dst_row, weight, rbf, vec,
          W0, b0, Win_s, Win_v, Wf1, bf1, Wf2, bf2, W1_s, W1_v, W2_s, W2_v, out):
    sum0 = nc.dram_tensor("sum0", (NP + TRASH, D), F32, kind="Internal").ap()
    sum1 = nc.dram_tensor("sum1", (NP + TRASH, D), F32, kind="Internal").ap()
    x1_d = nc.dram_tensor("x1_d", (NP, D), F32, kind="Internal").ap()

    with ExitStack() as ctx:
        def sb(name, shape, dt=F32):
            return ctx.enter_context(nc.sbuf_tensor(name, shape, dt))

        def sem(name):
            return ctx.enter_context(nc.semaphore(name))

        def ring(name, n, shape, dt=F32):
            return [sb(f"{name}{i}", shape, dt) for i in range(n)]

        bank = [ctx.enter_context(nc.psum_tensor(f"bank{i}", [P, 512], F32)) for i in range(8)]

        zeros = sb("zeros", [P, 1024])
        ident_i = sb("ident_i", [P, P], I32)
        iota_f = sb("iota_f", [P, 256])
        iota_i = sb("iota_i", [P, 256], I32)
        lane_i = sb("lane_i", [P, 2], I32)
        lane = sb("lane", [P, 2])
        trash_i = sb("trash_i", [P, T], I32)
        ident = sb("ident", [P, P])
        before = sb("before", [P, 2, 256])
        src_i = sb("src_i", [P, T], I32)
        dst_i = sb("dst_i", [P, T], I32)
        part_i = sb("part_i", [P, 4, T], I32)
        part = sb("part", [P, 4, T])
        src_f = sb("src_f", [P, T])
        dst_f = sb("dst_f", [P, T])
        trash = sb("trash", [P, T])
        to_trash_src = sb("to_trash_src", [P, T])
        to_trash_dst = sb("to_trash_dst", [P, T])
        ew = sb("ew", [P, T])
        coef = sb("coef", [P, T])
        dsrc = sb("dsrc", [P, T])
        deg = sb("deg", [P, T])
        degm = sb("degm", [P, T])
        degs = sb("degs", [P, T])
        degt = sb("degt", [P, T])
        dis = sb("dis", [P, T])
        rij = sb("rij", [P, T, 3])
        rsq = sb("rsq", [P, T, 3])
        rn = sb("rn", [P, T])
        Y = sb("Y", [P, T, 3])
        W0_s = sb("W0_s", [P, 4, D])
        b0_s = sb("b0_s", [P, D])
        Wins = sb("Wins", [P, C])
        Winv = sb("Winv", [P, C])
        Wf1_s = sb("Wf1_s", [RBF, C])
        bf1_c = sb("bf1_c", [P, 1])
        Wf2_s = sb("Wf2_s", [P, 512])
        bf2_c = sb("bf2_c", [P, 4])
        W1s_r = sb("W1s_r", [P, 2, C])
        W1v_r = sb("W1v_r", [P, 2, C])
        W1s_s = sb("W1s_s", [P, 2, C])
        W1vT = sb("W1vT", [P, 2, C])
        MV = sb("MV", [P, 2, C])
        W2s_r = sb("W2s_r", [P, C])
        W2s_s = sb("W2s_s", [P, C])
        W2v_r = sb("W2v_r", [P, C])

        hot_lo = ring("hot_lo", 2, [P, P])
        hot_hi = ring("hot_hi", 2, [P, T])
        srow = ring("srow", 2, [P, 512], I32)
        slow = ring("slow", 2, [P, 512], I32)
        hotT = ring("hotT", 2, [P, 512])
        junk80 = sb("junk80", [P, 8, T])
        trow = ring("trow", 2, [P, 256], I32)
        G = ring("G", 4, [P, D])
        M = ring("M", 4, [P, 256])
        R = ring("R", 4, [P, D])
        gidx = ring("gidx", 4, [P, 1], I32)
        sidx = ring("sidx", 4, [P, 1], I32)
        junk = ring("junk", 4, [P, 256])
        dup = ring("dup", 4, [P, 1])
        off = ring("off", 4, [P, 1])
        node_mem = ring("node_mem", 4, [P, 7 * D])
        sl, xl, zl, zT, pre, res, x1 = ([b[:, q * D:(q + 1) * D] for b in node_mem] for q in range(7))
        stat = ring("stat", 4, [P, 6])
        mv = ring("mv", 4, [P, 2])
        tiny = ring("tiny", 4, [P, 8])
        trow3 = ring("trow3", 4, [P, P], I32)
        fT = ring("fT", 4, [RBF, P])
        G3 = ring("G3", 4, [P, D])
        proj = ring("proj", 4, [P, P])
        rawT = ring("rawT", 2, [P, 640])
        hx = ring("hx", 2, [P, 3, P])
        hr = ring("hr", 2, [P, P])
        h = ring("h", 2, [P, P])
        feat = ring("feat", 2, [P, 640])
        m = ring("m", 2, [P, 768])
        msg = ring("msg", 2, [P, 640])
        M3 = ring("M3", 4, [P, P])
        R3 = ring("R3", 4, [P, D])
        gidx3 = ring("gidx3", 4, [P, 1], I32)
        sidx3 = ring("sidx3", 4, [P, 1], I32)
        dup3 = ring("dup3", 4, [P, 1])
        off3 = ring("off3", 4, [P, 1])
        def pairs(lo, hi):
            return [b[:, lo:hi].rearrange("p (k d) -> p k d", k=2) for b in node_mem]

        al = pairs(0, 2 * D)
        y_out = pairs(2 * D, 4 * D)
        ssum = pairs(4 * D, 4 * D + 2 * C)
        sr = pairs(4 * D + 2 * C, 5 * D)
        sx = [b[:, 5 * D:5 * D + 6 * C].rearrange("p (q k d) -> p q k d", q=3, k=2) for b in node_mem]
        sp = pairs(5 * D + 6 * C, 7 * D)
        spT = ring("spT", 4, [P, 2, C])
        xs = ring("xs", 4, [P, 2, C])
        stat4 = ring("stat4", 4, [P, 2, 6])
        mv4 = ring("mv4", 4, [P, 2, 2])
        tiny4 = ring("tiny4", 4, [P, 8, 2])

        s_load = sem("s_load")
        s_loadw = sem("s_loadw")
        s_zero = sem("s_zero")
        s_zero0 = sem("s_zero0")
        s_zero1 = sem("s_zero1")
        s_iota = sem("s_iota")
        s_const = sem("s_const")
        s_deg_hot = sem("s_deg_hot")
        s_deg_mm = sem("s_deg_mm")
        s_sqrt = sem("s_sqrt")
        s_srow = [sem(f"s_srow{i}") for i in range(2)]
        s_low = sem("s_low")
        s_hotT = sem("s_hotT")
        s_look = sem("s_look")
        s_pick = sem("s_pick")
        s_wprep = sem("s_wprep")
        s_wT = sem("s_wT")
        s_wTc = sem("s_wTc")
        s_wmv = sem("s_wmv")
        e_trow = [sem(f"e_trow{i}") for i in range(2)]
        e_gidx = sem("e_gidx")
        e_gather = [sem(f"e_gather{i}") for i in range(4)]
        e_M = sem("e_M")
        e_idx = sem("e_idx")
        e_mm = sem("e_mm")
        e_ev = sem("e_ev")
        e_scat = [sem(f"e_scat{i}") for i in range(4)]
        n_sl = [sem(f"n_sl{i}") for i in range(4)]
        n_xl = [sem(f"n_xl{i}") for i in range(4)]
        n_z = sem("n_z")
        n_tr = sem("n_tr")
        n_zT = sem("n_zT")
        n_mm = sem("n_mm")
        n_res = sem("n_res")
        n_rs = sem("n_rs")
        n_rstd = sem("n_rstd")
        n_x1 = sem("n_x1")
        n_st = [sem(f"n_st{i}") for i in range(4)]
        f_trow = [sem(f"f_trow{i}") for i in range(4)]
        f_fT = [sem(f"f_fT{i}") for i in range(4)]
        f_gidx = sem("f_gidx")
        f_gather = [sem(f"f_gather{i}") for i in range(4)]
        f_proj = sem("f_proj")
        f_tr = sem("f_tr")
        f_hmm = sem("f_hmm")
        f_rawT = sem("f_rawT")
        f_soft = sem("f_soft")
        f_h = sem("f_h")
        f_wv = sem("f_wv")
        f_feat = sem("f_feat")
        f_m = sem("f_m")
        f_o = sem("f_o")
        f_us = sem("f_us")
        f_msg = sem("f_msg")
        f_M = sem("f_M")
        f_idx = sem("f_idx")
        f_mm = sem("f_mm")
        f_ev = sem("f_ev")
        f_scat = [sem(f"f_scat{i}") for i in range(4)]
        g_ss = [sem(f"g_ss{i}") for i in range(4)]
        g_al = [sem(f"g_al{i}") for i in range(4)]
        g_xs = [sem(f"g_xs{i}") for i in range(4)]
        g_soft = sem("g_soft")
        g_sr = sem("g_sr")
        g_sp = sem("g_sp")
        g_tr = sem("g_tr")
        g_spT = sem("g_spT")
        g_mm = sem("g_mm")
        g_res = sem("g_res")
        g_rs = sem("g_rs")
        g_rstd = sem("g_rstd")
        g_y = sem("g_y")
        g_st = [sem(f"g_st{i}") for i in range(4)]
        hold = {e: sem(f"hold_{e}") for e in ("pool", "sync", "vector")}

        def held(eng, s, value):
            if not isinstance(value, int) or value > 0:
                eng.wait_ge(s, value)
                eng.sem_inc(hold["pool" if eng is nc.gpsimd else "sync" if eng is nc.sync else "vector"], 1)

        K_M, K_IDX = 1, 3
        K_RES, K_RSTD = 5, 4
        K_RES4 = 6
        K_PROJ, K_SOFT, K_PROD, K_MSG = 3, 4, 4, 3

        block = ctx.enter_context(nc.Block())

        @block.sync
        def _(sp_):
            for dst, src in ((src_i, src_cols), (dst_i, dst_cols), (ew, weight)):
                sp_.dma_start(dst[:, :], src).then_inc(s_load, 16)
            sp_.dma_start(rij[:, :, :], vec).then_inc(s_load, 16)

            def load_srow(g, u):
                held(sp_, s_low, g - 1)
                sp_.dma_start(srow[u][:, :], src_row[:, bass.ds(g * 512, 512)].broadcast_to([P, 512])) \
                   .then_inc(s_srow[u], 16)

            for g in range(2):
                load_srow(g, g)
            for dst, src in (
                (W0_s[:, :, :], W0.rearrange("(c p) n -> p c n", p=P)), (b0_s[:, :], b0.broadcast_to([P, D])),
                (Wins[:, :], Win_s), (Winv[:, :], Win_v), (Wf1_s[:, :], Wf1),
                (bf1_c[:, :], bf1), (Wf2_s[:, :], Wf2[:, 0:512]), (bf2_c[:, :], bf2),
                (W1s_r[:, :, :], W1_s.rearrange("(f k) c -> f k c", k=2)),
                (W1v_r[:, :, :], W1_v.rearrange("(f k) c -> f k c", k=2)),
                (W2s_r[:, :], W2_s), (W2v_r[:, :], W2_v),
            ):
                sp_.dma_start(dst, src).then_inc(s_loadw, 16)

            with sp_.Fori(1, T // 8) as j:
                for u in range(2):
                    load_srow(j * 2 + u, u)

            def load_trow(g, u):
                held(sp_, e_M, 2 * (g - 1))
                held(sp_, e_idx, 2 * K_IDX * (g - 1))
                sp_.dma_start(trow[u][:, :], dst_row[:, bass.ds(g * 256, 256)].broadcast_to([P, 256])) \
                   .then_inc(e_trow[u], 16)

            for g in range(2):
                load_trow(g, g)
            with sp_.Fori(1, T // 4) as j:
                for u in range(2):
                    load_trow(j * 2 + u, u)

            for u in range(4):
                sp_.wait_ge(e_scat[u], 16 * (T // 4))

            def nodes0(s, u):
                if live(s, 0):
                    held(sp_, n_z, s - 3)
                    sp_.dma_start(sl[u][:, :], rows(sum0, s)).then_inc(n_sl[u], 16)
                    held(sp_, n_res, K_RES * (s - 3))
                    sp_.dma_start(xl[u][:, :], rows(x, s)).then_inc(n_xl[u], 16)

            skewed(sp_, nodes0, 0, 4)

            def edges1(s, u):
                if live(s, 0):
                    held(sp_, f_hmm, s - 3)
                    sp_.dma_start(fT[u][:, :], rbf[:, bass.ds(s * P, P)]).then_inc(f_fT[u], 16)
                    held(sp_, f_M, s - 3)
                    held(sp_, f_idx, K_IDX * (s - 3))
                    sp_.dma_start(trow3[u][:, :], src_row[:, bass.ds(s * P, P)].broadcast_to([P, P])) \
                       .then_inc(f_trow[u], 16)

            skewed(sp_, edges1, 0, 4)

            for u in range(4):
                sp_.wait_ge(f_scat[u], 16 * (T // 4))

            def nodes1(s, u):
                if live(s, 0, T2):
                    held(sp_, g_soft, 3 * (s - 3))
                    held(sp_, g_sr, s - 3)
                    sp_.dma_start(ssum[u][:, :, :], pair_rows(sum1, s, 0, C)).then_inc(g_ss[u], 16)
                if live(s, 2, T2):
                    t, a = s - 2, (u - 2) % 4
                    held(sp_, g_y, 2 * (t - 3))
                    sp_.dma_start(al[a][:, :, C:D], pair_rows(sum1, t, C, D)).then_inc(g_al[a], 16)
                    held(sp_, g_res, K_RES4 * (t - 3))
                    sp_.dma_start(xs[a][:, :, :], pair_rows(x1_d, t, 0, C)).then_inc(g_xs[a], 16)

            skewed(sp_, nodes1, 2, 8, steps=T2)

        @block.gpsimd
        def _(pool):
            pool.iota(iota_i[:, :], [[1, 256]], base=0, channel_multiplier=0).then_inc(s_iota, 1)
            pool.iota(lane_i[:, :], [[P, 2]], base=0, channel_multiplier=1).then_inc(s_iota, 1)
            pool.iota(ident_i[:, :], [[1, P]], base=0, channel_multiplier=-1).then_inc(s_iota, 1)
            pool.iota(trash_i[:, :], [[0, T // 2], [P, 2]], base=NP, channel_multiplier=1).then_inc(s_iota, 1)

            def gather0(g, gp):
                for u in range(2):
                    k = 2 * gp + u
                    held(pool, e_gidx, 2 * g + u + 1)
                    held(pool, e_mm, g - 1)
                    pool.indirect_dma_start(G[k][:, :], None, x, bass.IndirectOffsetOnAxis(ap=gidx[k][:, :], axis=0)) \
                        .then_inc(e_gather[k], 16)

            def scatter0(g, gp, n):
                for u in range(2):
                    k = 2 * gp + u
                    held(pool, e_idx, K_IDX * (2 * g + u + 1))
                    held(pool, e_ev, 2 * g + u + 1)
                    if u == 0:
                        for v in range(2):
                            held(pool, e_scat[2 * (1 - gp) + v], 16 * (n + gp))
                    pool.indirect_dma_start(sum0, bass.IndirectOffsetOnAxis(ap=sidx[k][:, :], axis=0), R[k][:, :], None,
                                            compute_op=ALU.add).then_inc(e_scat[k], 16)

            gather0(0, 0)
            held(pool, s_zero0, 16 * 41)
            gather0(1, 1)
            scatter0(0, 0, 0)
            with pool.Fori(1, T // 4) as j:
                gather0(2 * j, 0)
                scatter0(2 * j - 1, 1, j - 1)
                gather0(2 * j + 1, 1)
                scatter0(2 * j, 0, j)
            scatter0(T // 2 - 1, 1, T // 4 - 1)

            for u in range(4):
                held(pool, n_st[u], 32 * (T // 4))
            held(pool, s_zero1, 16 * 22)

            def edges1(s, u):
                if live(s, 1):
                    t, a = s - 1, (u - 1) % 4
                    held(pool, f_gidx, t + 1)
                    held(pool, f_tr, t - 3)
                    held(pool, f_proj, K_PROJ * (t - 3))
                    pool.indirect_dma_start(G3[a][:, :], None, x1_d, bass.IndirectOffsetOnAxis(ap=gidx3[a][:, :], axis=0)) \
                        .then_inc(f_gather[a], 16)
                if live(s, 8):
                    t = s - 8
                    held(pool, f_idx, K_IDX * (t + 1))
                    held(pool, f_ev, t + 1)
                    held(pool, f_scat[u - 1], 16 * (turn(t, u, 4) + (u > 0)))
                    pool.indirect_dma_start(sum1, bass.IndirectOffsetOnAxis(ap=sidx3[u][:, :], axis=0), R3[u][:, :], None,
                                            compute_op=ALU.add).then_inc(f_scat[u], 16)

            skewed(pool, edges1, 8, 12)

        @block.scalar
        def _(act):
            act.wait_ge(s_zero, 1)
            with act.Fori(0, 41) as j:
                act.dma_start(sum0[bass.ds(j * 256, 256), :].rearrange("(p r) d -> p (r d)", r=2), zeros[:, :]) \
                   .then_inc(s_zero0, 16)
            act.wait_ge(s_const, 11)
            act.activation(degs[:, :], degm[:, :], ACT.Sqrt).then_inc(s_sqrt, 1)
            act.activation(rn[:, :], rsq[:, :, 0], ACT.Sqrt).then_inc(s_sqrt, 1)
            with act.Fori(0, 20) as j:
                act.dma_start(sum1[bass.ds(j * 512, 512), 0:C].rearrange("(p r) d -> p r d", r=4),
                              zeros[:, 0:512].rearrange("p (r d) -> p r d", r=4)).then_inc(s_zero1, 16)
            for q in range(2):
                act.dma_start(sum1[NP + q * P:NP + (q + 1) * P, :], zeros[:, 0:D]).then_inc(s_zero1, 16)

            act.wait_ge(s_wT, 1)
            act.copy(W1vT[:, :, :], bank[7][:, 0:256].rearrange("p (k c) -> p k c", k=2)).then_inc(s_wTc, 1)
            act.wait_ge(s_wmv, 1)
            act.mul(MV[:, 0, :], bank[7][:, 256:384], 1.0 / (16.0 * C)).then_inc(s_wTc, 1)
            act.mul(MV[:, 1, :], bank[7][:, 384:512], Y0 / (16.0 * C)).then_inc(s_wTc, 1)

            def evac0(g, gp, n):
                for u in range(2):
                    k = 2 * gp + u
                    act.wait_ge(e_mm, g + 1)
                    wait(act, e_scat[k], 16 * n)
                    act.copy(R[k][:, :], bank[k][:, :]).then_inc(e_ev, 1)

            for g in range(2):
                evac0(g, g, 0)
            with act.Fori(1, T // 4) as j:
                for gp in range(2):
                    evac0(2 * j + gp, gp, j)

            act.preload_act_table_set("natural_log_exp_and_others")

            def nodes0(s, u):
                if live(s, 0):
                    act.wait_ge(n_tr, s + 1)
                    wait(act, n_mm, s - 3)
                    act.copy(zT[u][:, :], bank[u][:, :]).then_inc(n_zT, 1)
                if live(s, 4):
                    t = s - 4
                    act.wait_ge(n_rstd, K_RSTD * (t + 1))
                    wait(act, n_st[u], 32 * turn(t, u, 4))
                    act.activation(x1[u][:, :], res[u][:, :], ACT.Identity, bias=tiny[u][:, 6:7], scale=tiny[u][:, 5:6]) \
                       .then_inc(n_x1, 1)
                if live(s, 3):
                    t, a = s - 3, (u - 3) % 4
                    act.wait_ge(n_res, K_RES * (t + 1))
                    act.activation(tiny[a][:, 1:2], tiny[a][:, 0:1], ACT.Ln).then_inc(n_rs, 1)
                    act.wait_ge(n_rs, 2 * t + 1)
                    act.activation(tiny[a][:, 2:3], tiny[a][:, 1:2], ACT.Exp, scale=-0.5).then_inc(n_rs, 1)
                if live(s, 4):
                    t = s - 4
                    act.wait_ge(n_x1, t + 1)
                    act.dma_start(rows(x1_d, t), x1[u][:, :]).then_inc(n_st[u], 16)
                    act.dma_start(sum1[bass.ds(t * P, P), C:D], x1[u][:, C:D]).then_inc(n_st[u], 16)

            skewed(act, nodes0, 4, 8)

            def edges1(s, u):
                if live(s, 4):
                    t, b = s - 4, u % 2
                    act.wait_ge(f_tr, t + 1)
                    wait(act, f_wv, t - 1)
                    act.copy(rawT[b][:, 0:512], bank[0][:, :]).then_inc(f_rawT, 1)
                    act.wait_ge(f_hmm, t + 1)
                    act.copy(rawT[b][:, 512:640], bank[1][:, 0:P]).then_inc(f_rawT, 1)
                    wait(act, f_h, t - 1)
                    st = Stage(f_soft, t, K_SOFT)
                    st.mark(act.activation(hx[b][:, 0, :], bank[1][:, P:2 * P], ACT.Abs, bias=bf1_c[:, :]))
                    st.mark(act.activation(hr[b][:, :], bank[1][:, P:2 * P], ACT.Relu, bias=bf1_c[:, :]))
                    st.settle(act)
                    st.mark(act.activation(hx[b][:, 1, :], hx[b][:, 0, :], ACT.Exp, scale=-1.0))
                    st.settle(act)
                    st.mark(act.activation(hx[b][:, 2, :], hx[b][:, 1, :], ACT.Ln, bias=1.0))
                if live(s, 5):
                    t, b = s - 5, (u - 5) % 2
                    act.wait_ge(f_wv, t + 1)
                    wait(act, f_m, K_PROD * (t - 1))
                    act.copy(feat[b][:, 0:512], bank[2][:, :]).then_inc(f_feat, 1)
                    act.copy(feat[b][:, 512:640], bank[3][:, 0:P]).then_inc(f_feat, 1)
                if live(s, 6):
                    t, b = s - 6, u % 2
                    act.wait_ge(f_o, t + 1)
                    wait(act, f_mm, t - 1)
                    act.copy(msg[b][:, 0:256], bank[5][:, 0:256]).then_inc(f_us, 1)
                if live(s, 7):
                    t, a = s - 7, (u - 7) % 4
                    act.wait_ge(f_mm, t + 1)
                    wait(act, f_scat[a], 16 * turn(t, a, 4))
                    act.copy(R3[a][:, :], bank[7][:, :]).then_inc(f_ev, 1)

            skewed(act, edges1, 7, 12)

            def nodes1(s, u):
                t, a = s - 5, (u - 5) % 4
                st = Stage(g_soft, s, 3)
                def normalise(k):
                    act.activation(y_out[a][:, k, :], al[a][:, k, :], ACT.Identity, bias=tiny4[a][:, 6, k:k + 1],
                                   scale=tiny4[a][:, 5, k:k + 1]).then_inc(g_y, 1)

                if live(s, 0, T2):
                    act.wait_ge(g_ss[u], 16 * (turn(s, u, 4) + 1))
                    wait(act, g_sp, s - 3)
                    st.mark(act.activation(sx[u][:, 0, :, :], ssum[u][:, :, :], ACT.Abs))
                if live(s, 5, T2):
                    act.wait_ge(g_rstd, K_RSTD * (t + 1))
                    wait(act, g_st[a], 16 * turn(t, a, 4))
                    normalise(0)
                if live(s, 0, T2):
                    st.settle(act)
                    st.mark(act.activation(sx[u][:, 1, :, :], sx[u][:, 0, :, :], ACT.Exp, scale=-1.0))
                if live(s, 5, T2):
                    normalise(1)
                if live(s, 0, T2):
                    st.settle(act)
                    st.mark(act.activation(sx[u][:, 2, :, :], sx[u][:, 1, :, :], ACT.Ln, bias=1.0))
                if live(s, 2, T2):
                    t2, b = s - 2, (u - 2) % 4
                    act.wait_ge(g_tr, t2 + 1)
                    wait(act, g_mm, t2 - 3)
                    act.copy(spT[b][:, :, :], bank[b][:, 0:256].rearrange("p (k c) -> p k c", k=2)).then_inc(g_spT, 1)
                if live(s, 4, T2):
                    t4 = s - 4
                    act.wait_ge(g_res, K_RES4 * (t4 + 1))
                    act.activation(tiny4[u][:, 1, :], tiny4[u][:, 0, :], ACT.Ln).then_inc(g_rs, 1)
                    act.wait_ge(g_rs, 2 * t4 + 1)
                    act.activation(tiny4[u][:, 2, :], tiny4[u][:, 1, :], ACT.Exp, scale=-0.5).then_inc(g_rs, 1)
                if live(s, 5, T2):
                    act.wait_ge(g_y, 2 * (t + 1))
                    act.dma_start(pair_rows(out, t, 0, D), y_out[a][:, :, :]).then_inc(g_st[a], 16)

            skewed(act, nodes1, 5, 12, steps=T2)
            for v in range(4):
                act.wait_ge(g_st[v], 16 * (T2 // 4))

        @block.vector
        def _(dve):
            count = [0]

            def link(ins):
                count[0] += 1
                ins.then_inc(s_const, 1)
                dve.wait_ge(s_const, count[0])

            dve.memset(zeros[:, :], 0.0).then_inc(s_zero, 1)
            dve.wait_ge(s_iota, 4)
            dve.tensor_copy(iota_f[:, :], iota_i[:, :])
            dve.tensor_copy(lane[:, :], lane_i[:, :])
            dve.tensor_copy(trash[:, :], trash_i[:, :])
            dve.wait_ge(s_load, 64)
            dve.tensor_copy(src_f[:, :], src_i[:, :])
            dve.tensor_copy(dst_f[:, :], dst_i[:, :])
            dve.tensor_scalar(part_i[:, 0, :], dst_i[:, :], 127, None, ALU.bitwise_and)
            dve.tensor_scalar(part_i[:, 1, :], dst_i[:, :], 7, None, ALU.logical_shift_right)
            dve.tensor_scalar(part_i[:, 2, :], src_i[:, :], 127, None, ALU.bitwise_and)
            dve.tensor_scalar(part_i[:, 3, :], src_i[:, :], 7, None, ALU.logical_shift_right)
            link(dve.tensor_scalar(ident[:, :], ident_i[:, :], 0.0, None, ALU.is_equal))
            dve.tensor_tensor(to_trash_src[:, :], trash[:, :], src_f[:, :], ALU.subtract)
            dve.tensor_tensor(to_trash_dst[:, :], trash[:, :], dst_f[:, :], ALU.subtract)
            for u in range(2):
                dve.tensor_scalar(before[:, u, :], iota_f[:, :], lane[:, u:u + 1], None, ALU.is_lt)
            link(dve.tensor_copy(part[:, :, :], part_i[:, :, :]))

            def hots(t, u):
                wait(dve, s_deg_mm, t)
                dve.tensor_scalar(hot_lo[u][:, :], iota_f[:, 0:P], part[:, 0, bass.ds(t, 1)], None, ALU.is_equal) \
                   .then_inc(s_deg_hot, 1)
                dve.tensor_scalar(hot_hi[u][:, :], iota_f[:, 0:T], part[:, 1, bass.ds(t, 1)], ew[:, bass.ds(t, 1)],
                                  ALU.is_equal, ALU.mult).then_inc(s_deg_hot, 1)

            for t in range(2):
                hots(t, t)
            with dve.Fori(1, T // 2) as j:
                for u in range(2):
                    hots(2 * j + u, u)

            dve.tensor_tensor(rsq[:, :, :], rij[:, :, :], rij[:, :, :], ALU.mult)
            dve.wait_ge(s_deg_mm, T + 1)
            link(dve.tensor_scalar(deg[:, :], bank[6][:, 0:T], 1.0, None, ALU.add))
            link(dve.tensor_scalar(degm[:, :], deg[:, :], 1e-34, None, ALU.max))
            link(dve.tensor_scalar(deg[:, :], deg[:, :], 0.0, None, ALU.is_gt))
            link(dve.tensor_tensor(rsq[:, :, 0], rsq[:, :, 0], rsq[:, :, 1], ALU.add))
            link(dve.tensor_tensor(rsq[:, :, 0], rsq[:, :, 0], rsq[:, :, 2], ALU.add))
            for q in range(2):
                k = Y0 / (16.0 * C ** 0.5) if q == 0 else 1.0 / (16.0 * C ** 0.5 * 3.0 ** 0.5)
                dve.wait_ge(s_loadw, 16 * 12)
                link(dve.tensor_scalar(W1s_s[:, q, :], W1s_r[:, q, :], k, None, ALU.mult))
            link(dve.tensor_scalar(W2s_s[:, :], W2s_r[:, :], 1.0 / C ** 0.5, None, ALU.mult))
            link(dve.tensor_copy(degt[:, :], degm[:, :]))
            dve.wait_ge(s_sqrt, 2)
            link(dve.reciprocal(dis[:, :], degs[:, :]))
            link(dve.reciprocal(rn[:, :], rn[:, :]))
            link(dve.tensor_tensor(degt[:, :], degt[:, :], dis[:, :], ALU.mult))
            link(dve.tensor_tensor(degt[:, :], degt[:, :], dis[:, :], ALU.mult))
            link(dve.tensor_scalar(degt[:, :], degt[:, :], -0.5, 1.5, ALU.mult, ALU.add))
            link(dve.tensor_tensor(dis[:, :], dis[:, :], degt[:, :], ALU.mult))
            link(dve.tensor_tensor(dis[:, :], dis[:, :], deg[:, :], ALU.mult))
            link(dve.scalar_tensor_tensor(Y[:, :, :], rij[:, :, :], Y1, rn[:, :].unsqueeze(2).broadcast_to([P, T, 3]),
                                          ALU.mult, ALU.mult))
            dve.sem_inc(s_pick, 1)

            def transposed_hots(g, u, n):
                dve.wait_ge(s_srow[u], 16 * (n + 1))
                wait(dve, s_hotT, g - 1)
                dve.tensor_scalar(slow[u][:, :], srow[u][:, :], 127, None, ALU.bitwise_and).then_inc(s_low, 1)
                dve.wait_ge(s_low, g + 1)
                wait(dve, s_look, g - 1)
                dve.tensor_scalar(hotT[u][:, :], slow[u][:, :], lane[:, 0:1], None, ALU.is_equal).then_inc(s_hotT, 1)

            def pick(g, u):
                dve.wait_ge(s_look, g + 1)
                for q in range(4):
                    t = 4 * g + q
                    ins = dve.scalar_tensor_tensor(junk80[:, 4 * u + q, :], iota_f[:, 0:T], part[:, 3, bass.ds(t, 1)],
                                                   bank[u][:, q * T:(q + 1) * T], ALU.is_equal, ALU.mult,
                                                   accum_out=dsrc[:, bass.ds(t, 1)])
                ins.then_inc(s_pick, 1)

            transposed_hots(0, 0, 0)
            transposed_hots(1, 1, 0)
            pick(0, 0)
            with dve.Fori(1, T // 8) as j:
                transposed_hots(2 * j, 0, j)
                pick(2 * j - 1, 1)
                transposed_hots(2 * j + 1, 1, j)
                pick(2 * j, 0)
            pick(T // 4 - 1, 1)
            dve.wait_ge(s_pick, T // 4 + 1)
            link(dve.tensor_tensor(coef[:, :], ew[:, :], dsrc[:, :], ALU.mult))

            def combine0(g, gp, n):
                for u in range(2):
                    k = 2 * gp + u
                    wait(dve, e_gather[k], 16 * n)
                    dve.tensor_scalar(gidx[k][:, :], src_i[:, bass.ds(2 * g + u, 1)], 0.0, None, ALU.add).then_inc(e_gidx, 1)
                dve.wait_ge(e_trow[gp], 16 * (n + 1))
                for u in range(2):
                    k, t = 2 * gp + u, 2 * g + u
                    wait(dve, e_mm, g - 1)
                    dve.tensor_scalar(M[k][:, :], trow[gp][:, :], dst_f[:, bass.ds(t, 1)], coef[:, bass.ds(t, 1)],
                                      ALU.is_equal, ALU.mult).then_inc(e_M, 1)
                for u in range(2):
                    k, t = 2 * gp + u, 2 * g + u
                    st = Stage(e_idx, t, K_IDX)
                    st.mark(dve.scalar_tensor_tensor(junk[k][:, :], trow[gp][:, :], dst_f[:, bass.ds(t, 1)], before[:, u, :],
                                                     ALU.is_equal, ALU.mult, accum_out=dup[k][:, :]))
                    st.settle(dve)
                    st.mark(dve.tensor_scalar(off[k][:, :], dup[k][:, :], 1.0, to_trash_dst[:, bass.ds(t, 1)], ALU.min, ALU.mult))
                    st.settle(dve)
                    wait(dve, e_scat[k], 16 * n)
                    st.mark(dve.tensor_scalar(sidx[k][:, :], off[k][:, :], dst_f[:, bass.ds(t, 1)], None, ALU.add))

            for g in range(2):
                combine0(g, g, 0)
            with dve.Fori(1, T // 4) as j:
                for gp in range(2):
                    combine0(2 * j + gp, gp, j)

            def rstd(st, w, mvar):
                def square():
                    st.mark(dve.tensor_scalar(w[:, 3:4], w[:, 2:3], w[:, 2:3], w[:, 0:1], ALU.mult, ALU.mult))

                def factor():
                    st.settle(dve)
                    st.mark(dve.tensor_scalar(w[:, 4:5], w[:, 3:4], -0.5, 1.5, ALU.mult, ALU.add))

                def root():
                    st.settle(dve)
                    st.mark(dve.tensor_tensor(w[:, 5:6], w[:, 4:5], w[:, 2:3], ALU.mult))

                def shift():
                    st.settle(dve)
                    st.mark(dve.tensor_scalar(w[:, 6:7], mvar[:, 0:1], w[:, 5:6], -1.0, ALU.mult, ALU.mult))

                return square, factor, root, shift

            def nodes0(s, u):
                t, a = s - 2, (u - 2) % 4
                st, sr_ = Stage(n_res, t, K_RES), Stage(n_rstd, s - 4, K_RSTD)
                steps = rstd(sr_, tiny[u], mv[u])
                if live(s, 0):
                    n = turn(s, u, 4)
                    dve.wait_ge(n_sl[u], 16 * (n + 1))
                    dve.wait_ge(n_xl[u], 16 * (n + 1))
                    wait(dve, n_tr, s - 3)
                    dve.scalar_tensor_tensor(zl[u][:, :], xl[u][:, :], dis[:, bass.ds(s, 1)], sl[u][:, :],
                                             ALU.mult, ALU.add).then_inc(n_z, 1)
                if live(s, 4):
                    dve.wait_ge(n_rs, 2 * (s - 3))
                    steps[0]()
                if live(s, 2):
                    dve.wait_ge(n_mm, t + 1)
                    st.mark(dve.scalar_tensor_tensor(pre[a][:, :], bank[4 + a][:, :], dis[:, bass.ds(t, 1)], b0_s[:, :],
                                                     ALU.mult, ALU.add))
                if live(s, 4):
                    steps[1]()
                if live(s, 2):
                    st.settle(dve)
                    wait(dve, n_x1, t - 3)
                    st.mark(dve.scalar_tensor_tensor(res[a][:, :], pre[a][:, :], 0.0, xl[a][:, :], ALU.max, ALU.add))
                if live(s, 4):
                    steps[2]()
                if live(s, 2):
                    st.settle(dve)
                    st.mark(dve.bn_stats(stat[a][:, :], res[a][:, :]))
                if live(s, 4):
                    steps[3]()
                if live(s, 2):
                    held(dve, n_res, st.reached())
                    st.mark(dve.bn_aggr(mv[a][:, :], stat[a][:, :]))
                    st.settle(dve)
                    st.mark(dve.tensor_scalar(tiny[a][:, 0:1], mv[a][:, 1:2], EPS, None, ALU.add))

            skewed(dve, nodes0, 4, 8)

            def edges1(s, u):
                if live(s, 0):
                    wait(dve, f_gather[u], 16 * turn(s, u, 4))
                    dve.tensor_scalar(gidx3[u][:, :], dst_i[:, bass.ds(s, 1)], 0.0, None, ALU.add).then_inc(f_gidx, 1)
                t, a = s - 3, (u - 3) % 4
                sj = Stage(f_proj, t, K_PROJ)
                gv = G3[a][:, C:D].rearrange("p (c i) -> p c i", i=3)
                tm, b = s - 6, (u - 6) % 4
                si = Stage(f_idx, tm, K_IDX)
                if live(s, 3):
                    dve.wait_ge(f_gather[a], 16 * (turn(t, a, 4) + 1))
                    wait(dve, f_tr, t - 3)
                    sj.mark(dve.tensor_scalar(proj[a][:, :], gv[:, :, 0], Y[:, bass.ds(t, 1), 0], None, ALU.mult))
                if live(s, 6):
                    dve.wait_ge(f_trow[b], 16 * (turn(tm, b, 4) + 1))
                    si.mark(dve.scalar_tensor_tensor(junk[b][:, 0:P], trow3[b][:, :], src_f[:, bass.ds(tm, 1)],
                                                     before[:, 0, 0:P], ALU.is_equal, ALU.mult, accum_out=dup3[b][:, :]))
                if live(s, 3):
                    sj.settle(dve)
                    sj.mark(dve.scalar_tensor_tensor(proj[a][:, :], gv[:, :, 1], Y[:, bass.ds(t, 1), 1], proj[a][:, :],
                                                     ALU.mult, ALU.add))
                if live(s, 6):
                    wait(dve, f_mm, tm - 3)
                    dve.tensor_scalar(M3[b][:, :], trow3[b][:, :], src_f[:, bass.ds(tm, 1)], ew[:, bass.ds(tm, 1)],
                                      ALU.is_equal, ALU.mult).then_inc(f_M, 1)
                if live(s, 3):
                    sj.settle(dve)
                    sj.mark(dve.scalar_tensor_tensor(proj[a][:, :], gv[:, :, 2], Y[:, bass.ds(t, 1), 2], proj[a][:, :],
                                                     ALU.mult, ALU.add))
                if live(s, 6):
                    si.settle(dve)
                    si.mark(dve.tensor_scalar(off3[b][:, :], dup3[b][:, :], 1.0, to_trash_src[:, bass.ds(tm, 1)],
                                              ALU.min, ALU.mult))
                if live(s, 4):
                    t, c = s - 4, u % 2
                    wait(dve, f_wv, t - 1)
                    dve.wait_ge(f_soft, K_SOFT * (t + 1))
                    dve.scalar_tensor_tensor(h[c][:, :], hx[c][:, 2, :], -LOG2, hr[c][:, :], ALU.add, ALU.add).then_inc(f_h, 1)
                if live(s, 6):
                    si.settle(dve)
                    wait(dve, f_scat[b], 16 * turn(tm, b, 4))
                    si.mark(dve.tensor_scalar(sidx3[b][:, :], off3[b][:, :], src_f[:, bass.ds(tm, 1)], None, ALU.add))
                if live(s, 5):
                    t, c = s - 5, (u - 5) % 2
                    dve.wait_ge(f_wv, t + 1)
                    dve.wait_ge(f_feat, 2 * (t + 1))
                    wait(dve, f_o, t - 1)
                    st = Stage(f_m, t, K_PROD)
                    f_s, f_z = feat[c][:, 512:640], feat[c][:, 384:512]
                    for q, fe in ((0, f_s), (1, f_z), (2, f_s)):
                        st.mark(dve.scalar_tensor_tensor(m[c][:, q * P:(q + 1) * P], bank[4][:, q * P:(q + 1) * P],
                                                         bf2_c[:, q:q + 1], fe, ALU.add, ALU.mult))
                    st.mark(dve.scalar_tensor_tensor(
                        m[c][:, 384:768].rearrange("p (i e) -> p i e", i=3),
                        bank[4][:, 384:512].unsqueeze(1).broadcast_to([P, 3, P]), bf2_c[:, 3:4],
                        feat[c][:, 0:384].rearrange("p (i e) -> p i e", i=3), ALU.add, ALU.mult))
                if live(s, 6):
                    c = u % 2
                    dve.wait_ge(f_us, tm + 1)
                    dve.wait_ge(f_o, tm + 1)
                    st = Stage(f_msg, tm, K_MSG)
                    mo = msg[c][:, 256:640].rearrange("p (c i) -> p c i", i=3)
                    for i in range(3):
                        st.mark(dve.scalar_tensor_tensor(mo[:, :, i], msg[c][:, 0:P], Y[:, bass.ds(tm, 1), i],
                                                         bank[6][:, i * P:(i + 1) * P], ALU.mult, ALU.add))

            skewed(dve, edges1, 6, 12)

            def nodes1(s, u):
                t5, a5 = s - 5, (u - 5) % 4
                w = tiny4[a5]
                sv = Stage(g_rstd, t5, K_RSTD)
                t1, a1 = s - 1, (u - 1) % 4
                t3, a3 = s - 3, (u - 3) % 4
                st = Stage(g_res, t3, K_RES4)
                if live(s, 5, T2):
                    dve.wait_ge(g_rs, 2 * (t5 + 1))
                    sv.mark(dve.scalar_tensor_tensor(w[:, 3, :], w[:, 2, :], -0.5, w[:, 2, :], ALU.mult, ALU.mult))
                if live(s, 0, T2):
                    dve.wait_ge(g_ss[u], 16 * (turn(s, u, 4) + 1))
                    dve.tensor_scalar(sr[u][:, :, :], ssum[u][:, :, :], 0.0, -LOG2, ALU.max, ALU.add).then_inc(g_sr, 1)
                if live(s, 5, T2):
                    sv.settle(dve)
                    sv.mark(dve.tensor_tensor(w[:, 4, :], w[:, 3, :], w[:, 0, :], ALU.mult))
                if live(s, 3, T2):
                    dve.wait_ge(g_mm, t3 + 1)
                    dve.wait_ge(g_xs[a3], 16 * (turn(t3, a3, 4) + 1))
                    dve.wait_ge(g_al[a3], 16 * (turn(t3, a3, 4) + 1))
                    st.mark(dve.tensor_tensor(al[a3][:, :, 0:C], bank[4 + a3][:, 0:256].rearrange("p (k c) -> p k c", k=2),
                                              xs[a3][:, :, :], ALU.add))
                if live(s, 5, T2):
                    sv.settle(dve)
                    sv.mark(dve.scalar_tensor_tensor(w[:, 5, :], w[:, 4, :], 1.5, w[:, 2, :], ALU.add, ALU.mult))
                if live(s, 1, T2):
                    dve.wait_ge(g_sr, t1 + 1)
                    dve.wait_ge(g_soft, 3 * (t1 + 1))
                    wait(dve, g_tr, t1 - 3)
                    dve.tensor_tensor(sp[a1][:, :, :], sr[a1][:, :, :], sx[a1][:, 2, :, :], ALU.add).then_inc(g_sp, 1)
                if live(s, 5, T2):
                    sv.settle(dve)
                    sv.mark(dve.scalar_tensor_tensor(w[:, 6, :], mv4[a5][:, :, 0], -1.0, w[:, 5, :], ALU.mult, ALU.mult))
                if live(s, 3, T2):
                    st.settle(dve)
                    for k in range(2):
                        st.mark(dve.bn_stats(stat4[a3][:, k, :], al[a3][:, k, :]))
                    held(dve, g_y, 2 * (t3 - 3))
                    held(dve, g_res, st.reached())
                    for k in range(2):
                        st.mark(dve.bn_aggr(mv4[a3][:, k, :], stat4[a3][:, k, :]))
                    st.settle(dve)
                    st.mark(dve.tensor_scalar(tiny4[a3][:, 0, :], mv4[a3][:, :, 1], EPS, None, ALU.add))

            skewed(dve, nodes1, 5, 12, steps=T2)

        @block.tensor
        def _(pe):
            pe.wait_ge(s_zero, 1)
            pe.matmul(bank[6][:, 0:T], zeros[:, 0:P], zeros[:, 0:T], start=True, stop=False,
                      skip_group_check=True).then_inc(s_deg_mm, 1)

            def deg_mm(t, u):
                pe.wait_ge(s_deg_hot, 2 * t + 2)
                pe.matmul(bank[6][:, 0:T], hot_lo[u][:, :], hot_hi[u][:, :], start=False, stop=False,
                          skip_group_check=True).then_inc(s_deg_mm, 1)

            with pe.Fori(0, T // 2) as j:
                for u in range(2):
                    deg_mm(2 * j + u, u)

            def look(g, u):
                pe.wait_ge(s_hotT, g + 1)
                pe.wait_ge(s_pick, g if not isinstance(g, int) else max(g, 1))
                for q in range(4):
                    ins = pe.matmul(bank[u][:, q * T:(q + 1) * T], hotT[u][:, q * P:(q + 1) * P], dis[:, :],
                                    start=True, stop=True)
                ins.then_inc(s_look, 1)

            for g in range(2):
                look(g, g)
            with pe.Fori(1, T // 8) as j:
                for u in range(2):
                    look(2 * j + u, u)

            pe.wait_ge(s_loadw, 16 * 12)
            pe.wait_ge(s_const, 2)
            for q in range(2):
                ins = pe.transpose(bank[7][:, q * P:(q + 1) * P], W1v_r[:, q, :], ident[:, :])
            ins.then_inc(s_wT, 1)
            pe.wait_ge(s_wTc, 1)
            for q in range(2):
                ins = pe.matmul(bank[7][:, 256 + q * P:256 + (q + 1) * P], W1vT[:, q, :], W2v_r[:, :], start=True, stop=True)
            ins.then_inc(s_wmv, 1)

            def sums0(g, gp, n):
                for u in range(2):
                    pe.wait_ge(e_gather[2 * gp + u], 16 * (n + 1))
                pe.wait_ge(e_M, 2 * g + 2)
                wait(pe, e_ev, 2 * (g - 1))
                for u in range(2):
                    for v in range(2):
                        ins = pe.matmul(bank[2 * gp + u][:, :], M[2 * gp + v][:, u * P:(u + 1) * P], G[2 * gp + v][:, :],
                                        start=(v == 0), stop=(v == 1))
                ins.then_inc(e_mm, 1)

            pe.wait_ge(s_pick, T // 4 + 1)
            for g in range(2):
                sums0(g, g, 0)
            with pe.Fori(1, T // 4) as j:
                for gp in range(2):
                    sums0(2 * j + gp, gp, j)

            pe.wait_ge(e_ev, T)
            pe.wait_ge(s_loadw, 16 * 12)

            def nodes0(s, u):
                if live(s, 0):
                    pe.wait_ge(n_z, s + 1)
                    wait(pe, n_zT, s - 3)
                    for c in range(4):
                        ins = pe.transpose(bank[u][:, c * P:(c + 1) * P], zl[u][:, c * P:(c + 1) * P], ident[:, :])
                    ins.then_inc(n_tr, 1)
                if live(s, 1):
                    t, a = s - 1, (u - 1) % 4
                    pe.wait_ge(n_zT, t + 1)
                    wait(pe, n_res, K_RES * (t - 3))
                    for c in range(4):
                        ins = pe.matmul(bank[4 + a][:, :], zT[a][:, c * P:(c + 1) * P], W0_s[:, c, :],
                                        start=(c == 0), stop=(c == 3))
                    ins.then_inc(n_mm, 1)

            skewed(pe, nodes0, 1, 8)

            pe.wait_ge(n_zT, T)
            pe.wait_ge(n_res, K_RES * T)
            pe.wait_ge(s_wTc, 3)
            pe.wait_ge(s_const, 11)

            def edges1(s, u):
                if live(s, 4):
                    t, a = s - 4, u
                    pe.wait_ge(f_proj, K_PROJ * (t + 1))
                    pe.wait_ge(f_gather[a], 16 * (turn(t, a, 4) + 1))
                    wait(pe, f_rawT, 2 * t)
                    wait(pe, f_soft, K_SOFT * t)
                    gv = G3[a][:, C:D].rearrange("p (c i) -> p c i", i=3)
                    for i in range(3):
                        pe.transpose(bank[0][:, i * P:(i + 1) * P], gv[:, :, i], ident[:, :])
                    pe.transpose(bank[0][:, 384:512], proj[a][:, :], ident[:, :])
                    pe.transpose(bank[1][:, 0:P], G3[a][:, 0:C], ident[:, :]).then_inc(f_tr, 1)
                    pe.wait_ge(f_fT[a], 16 * (turn(t, a, 4) + 1))
                    pe.matmul(bank[1][:, P:2 * P], Wf1_s[:, :], fT[a][:, :], start=True, stop=True).then_inc(f_hmm, 1)
                if live(s, 5):
                    t, b = s - 5, (u - 5) % 2
                    pe.wait_ge(f_rawT, 2 * (t + 1))
                    wait(pe, f_feat, 2 * t)
                    pe.matmul(bank[2][:, :], Winv[:, :], rawT[b][:, 0:512], start=True, stop=True)
                    pe.matmul(bank[3][:, 0:P], Wins[:, :], rawT[b][:, 512:640], start=True, stop=True)
                    pe.wait_ge(f_h, t + 1)
                    wait(pe, f_m, K_PROD * t)
                    for q in range(4):
                        base = 256 * (q // 2) + q % 2
                        ins = pe.matmul(bank[4][:, q * P:(q + 1) * P], Wf2_s[:, base:base + 255:2], h[b][:, :],
                                        start=True, stop=True)
                    ins.then_inc(f_wv, 1)
                if live(s, 6):
                    t, b = s - 6, u % 2
                    pe.wait_ge(f_m, K_PROD * (t + 1))
                    wait(pe, f_us, t)
                    wait(pe, f_msg, K_MSG * t)
                    pe.matmul(bank[5][:, 0:P], m[b][:, 256:384], MV[:, 0, :], start=True, stop=True)
                    for q in range(2):
                        pe.matmul(bank[5][:, P:2 * P], m[b][:, q * P:(q + 1) * P], W1s_s[:, q, :], start=(q == 0), stop=(q == 1))
                    for i in range(3):
                        ins = pe.matmul(bank[6][:, i * P:(i + 1) * P], m[b][:, (3 + i) * P:(4 + i) * P], MV[:, 1, :],
                                        start=True, stop=True)
                    ins.then_inc(f_o, 1)
                if live(s, 7):
                    t, a, b = s - 7, (u - 7) % 4, (u - 7) % 2
                    pe.wait_ge(f_msg, K_MSG * (t + 1))
                    pe.wait_ge(f_us, t + 1)
                    pe.wait_ge(f_M, t + 1)
                    wait(pe, f_ev, t)
                    pe.matmul(bank[7][:, :], M3[a][:, :], msg[b][:, P:640], start=True, stop=True).then_inc(f_mm, 1)

            skewed(pe, edges1, 7, 12)

            pe.wait_ge(f_ev, T)

            def nodes1(s, u):
                if live(s, 1, T2):
                    t, a = s - 1, (u - 1) % 4
                    pe.wait_ge(g_sp, t + 1)
                    wait(pe, g_spT, t - 3)
                    for k in range(2):
                        ins = pe.transpose(bank[a][:, k * P:(k + 1) * P], sp[a][:, k, :], ident[:, :])
                    ins.then_inc(g_tr, 1)
                if live(s, 2, T2):
                    t, a = s - 2, (u - 2) % 4
                    pe.wait_ge(g_spT, t + 1)
                    wait(pe, g_res, K_RES4 * (t - 3))
                    for k in range(2):
                        ins = pe.matmul(bank[4 + a][:, k * C:(k + 1) * C], spT[a][:, k, :], W2s_s[:, :], start=True, stop=True)
                    ins.then_inc(g_mm, 1)

            skewed(pe, nodes1, 2, 8, steps=T2)


def kernel(x, src, dst, edge_attr_20, edge_attr_3, edge_weight, L0_gnn_W, L0_gnn_b, L1_gnn_W_in2f_s, L1_gnn_W_in2f_v,
           L1_gnn_Wf1, L1_gnn_bf1, L1_gnn_Wf2, L1_gnn_bf2, L1_gnn_W1_s, L1_gnn_W1_v, L1_gnn_W2_s, L1_gnn_W2_v):
    import concourse.bacc as bacc
    from concourse.bass_utils import run_bass_kernel_spmd

    def padded(a, value=0):
        a = np.asarray(a)
        out = np.full((NP,) + a.shape[1:], value, a.dtype)
        out[:N] = a
        return out

    def columns(a):
        return np.ascontiguousarray(np.moveaxis(a.reshape((T, P) + a.shape[1:]), 0, 1))

    ends = []
    for a in (src, dst):
        a = padded(a)
        a[N:] = np.arange(N, NP, dtype=a.dtype)
        ends.append(a)
    s, d = ends
    bf2 = np.asarray(L1_gnn_bf2)[:512].reshape(2, C, 2)
    arrays = {
        "x": padded(x),
        "src_cols": columns(s), "dst_cols": columns(d), "src_row": s.reshape(1, NP), "dst_row": d.reshape(1, NP),
        "weight": columns(padded(edge_weight)),
        "rbf": np.ascontiguousarray(padded(edge_attr_20).T),
        "vec": columns(padded(edge_attr_3, 1)),
        "W0": np.asarray(L0_gnn_W), "b0": np.asarray(L0_gnn_b).reshape(1, D),
        "Win_s": np.asarray(L1_gnn_W_in2f_s), "Win_v": np.asarray(L1_gnn_W_in2f_v),
        "Wf1": np.asarray(L1_gnn_Wf1), "bf1": np.asarray(L1_gnn_bf1).reshape(C, 1),
        "Wf2": np.asarray(L1_gnn_Wf2), "bf2": np.ascontiguousarray(bf2.transpose(1, 0, 2).reshape(C, 4)),
        "W1_s": np.asarray(L1_gnn_W1_s), "W1_v": np.asarray(L1_gnn_W1_v),
        "W2_s": np.asarray(L1_gnn_W2_s), "W2_v": np.asarray(L1_gnn_W2_v),
    }
    nc = bacc.Bacc("TRN2", target_bir_lowering=False, num_devices=1)
    args = [nc.dram_tensor(n, a.shape, mybir.dt.from_np(a.dtype), kind="ExternalInput").ap() for n, a in arrays.items()]
    args.append(nc.dram_tensor("out", (NP, D), F32, kind="ExternalOutput").ap())
    build(nc, *args)
    r = run_bass_kernel_spmd(nc, [arrays], core_ids=[0])
    return r.results[0]["out"][:N]
```

```python
from contextlib import ExitStack

import numpy as np

import concourse.bass as bass
from concourse import mybir

F32 = mybir.dt.float32
F32R = mybir.dt.float32r
I32 = mybir.dt.int32
ALU = mybir.AluOpType
ACT = mybir.ActivationFunctionType

P = 128
N = 10000
T = 80
NP = T * P
D = 512
C = 128
RBF = 20
T2 = T // 2
TRASH = 2 * P
EPS = 1e-5
LOG2 = float(np.log(2.0))
Y0 = float(1.0 / np.sqrt(4.0 * np.pi))
Y1 = float(np.sqrt(3.0 / (4.0 * np.pi)))


def skewed(eng, step, tail, lead, unroll=4, steps=T):
    for s in range(lead):
        step(s, s % unroll)
    with eng.Fori(lead // unroll, steps // unroll) as j:
        for u in range(unroll):
            step(j * unroll + u, u)
    for s in range(steps, steps + tail):
        step(s, s % unroll)


def live(s, lag, steps=T):
    return not isinstance(s, int) or 0 <= s - lag < steps


def turn(t, slot, n):
    return t // n if isinstance(t, int) else (t - slot) // n


def wait(eng, sem, value):
    if not isinstance(value, int) or value > 0:
        eng.wait_ge(sem, value)


class Stage:

    def __init__(self, sem, t, total):
        self.sem, self.t, self.total, self.n = sem, t, total, 0

    def mark(self, ins):
        self.n += 1
        ins.then_inc(self.sem, 1)

    def reached(self):
        return self.t * self.total + self.n

    def settle(self, eng):
        eng.wait_ge(self.sem, self.reached())


def rows(dram, t):
    return dram[bass.ds(t * P, P), :]


def pair_rows(dram, s, c0, c1):
    return dram[bass.ds(s * 2 * P, 2 * P), c0:c1].rearrange("(k p) d -> p k d", p=P)


def build(nc, x, src_cols, dst_cols, src_row, dst_row, weight, rbf, vec,
          W0, b0, Win_s, Win_v, Wf1, bf1, Wf2, bf2, W1_s, W1_v, W2_s, W2_v, out):
    sum0 = nc.dram_tensor("sum0", (NP + TRASH, D), F32, kind="Internal").ap()
    sum1 = nc.dram_tensor("sum1", (NP + TRASH, D), F32, kind="Internal").ap()
    x1_d = nc.dram_tensor("x1_d", (NP, D), F32, kind="Internal").ap()

    with ExitStack() as ctx:
        def sb(name, shape, dt=F32):
            return ctx.enter_context(nc.sbuf_tensor(name, shape, dt))

        def sem(name):
            return ctx.enter_context(nc.semaphore(name))

        def ring(name, n, shape, dt=F32):
            return [sb(f"{name}{i}", shape, dt) for i in range(n)]

        bank = [ctx.enter_context(nc.psum_tensor(f"bank{i}", [P, 512], F32)) for i in range(8)]

        zeros = sb("zeros", [P, 1024])
        ident_i = sb("ident_i", [P, P], I32)
        iota_f = sb("iota_f", [P, 256])
        iota_i = sb("iota_i", [P, 256], I32)
        lane_i = sb("lane_i", [P, 2], I32)
        lane = sb("lane", [P, 2])
        trash_i = sb("trash_i", [P, T], I32)
        ident = sb("ident", [P, P])
        eps_c = sb("eps_c", [P, 1])
        ident_r = sb("ident_r", [P, P], F32R)
        before = sb("before", [P, 2, 256])
        src_i = sb("src_i", [P, T], I32)
        dst_i = sb("dst_i", [P, T], I32)
        part_i = sb("part_i", [P, 4, T], I32)
        part = sb("part", [P, 4, T])
        src_f = sb("src_f", [P, T])
        dst_f = sb("dst_f", [P, T])
        trash = sb("trash", [P, T])
        to_trash_src = sb("to_trash_src", [P, T])
        to_trash_dst = sb("to_trash_dst", [P, T])
        ew = sb("ew", [P, T])
        coef = sb("coef", [P, T])
        dsrc = sb("dsrc", [P, T])
        deg = sb("deg", [P, T])
        degm = sb("degm", [P, T])
        degs = sb("degs", [P, T])
        degt = sb("degt", [P, T])
        dis = sb("dis", [P, T])
        rij = sb("rij", [P, T, 3])
        rsq = sb("rsq", [P, T, 3])
        rn = sb("rn", [P, T])
        Y = sb("Y", [P, T, 3])
        W0h = sb("W0h", [P, 4, D], F32R)
        W0l = sb("W0l", [P, 4, D], F32R)
        b0_s = sb("b0_s", [P, D])
        Wins = sb("Wins", [P, C])
        Winv = sb("Winv", [P, C])
        Wf1_s = sb("Wf1_s", [RBF, C])
        bf1_c = sb("bf1_c", [P, 1])
        Wf2_s = sb("Wf2_s", [P, 512])
        bf2_c = sb("bf2_c", [P, 4])
        W1s_r = sb("W1s_r", [P, 2, C])
        W1v_r = sb("W1v_r", [P, 2, C])
        W1s_s = sb("W1s_s", [P, 2, C])
        W1vT = sb("W1vT", [P, 2, C])
        MV = sb("MV", [P, 2, C])
        W2s_r = sb("W2s_r", [P, C])
        W2s_s = sb("W2s_s", [P, C])
        W2v_r = sb("W2v_r", [P, C])

        hot_lo = ring("hot_lo", 4, [P, P])
        hot_hi = ring("hot_hi", 4, [P, T])
        srow = ring("srow", 4, [P, 256], I32)
        slow = ring("slow", 4, [P, 256], I32)
        edge_mem = sb("edge_mem", [P, 5376])
        G_mem = sb("G_mem", [P, 8 * D])
        R_mem = sb("R_mem", [P, 8 * D])

        def views(start, n, width, mem=edge_mem):
            return [mem[:, start + i * width:start + (i + 1) * width] for i in range(n)]

        hotT = views(0, 4, 256)
        junk80 = sb("junk80", [P, 8, T])
        trow = ring("trow", 4, [P, 256], I32)
        G = views(0, 8, D, G_mem)
        M = views(1024, 8, 256)
        R = views(0, 8, D, R_mem)
        gidx = ring("gidx", 8, [P, 1], I32)
        sidx = ring("sidx", 8, [P, 1], I32)
        junk = views(3072, 8, 256)
        dup = ring("dup", 8, [P, 1])
        off = ring("off", 8, [P, 1])
        node_mem = ring("node_mem", 4, [P, 4 * D])
        sl, res, W0_s = ([b[:, q * D:(q + 1) * D] for b in node_mem] for q in range(3))
        xl = G
        z_hi, z_lo = (ring(name, 4, [P, D], F32R) for name in ("z_hi", "z_lo"))
        zT_hi, zT_lo = (ring(name, 2, [P, D], F32R) for name in ("zT_hi", "zT_lo"))
        stat = ring("stat", 4, [P, 6])
        mv = ring("mv", 4, [P, 2])
        tiny = ring("tiny", 4, [P, 8])
        trow3 = ring("trow3", 4, [P, P], I32)
        fT = ring("fT", 4, [RBF, P])
        G3, R3 = G[:4], R[:4]
        proj = ring("proj", 4, [P, P])
        rawT = views(0, 2, 640)
        hx = ring("hx", 2, [P, 3, P])
        hr = ring("hr", 2, [P, P])
        h = ring("h", 2, [P, P])
        feat = views(1280, 2, 640)
        m = views(2560, 2, 768)
        msg = views(4096, 2, 640)
        M3 = ring("M3", 4, [P, P], F32R)
        msg_hi, msg_lo = z_hi, z_lo
        junk3 = ring("junk3", 4, [P, P])
        gidx3 = ring("gidx3", 4, [P, 1], I32)
        sidx3 = ring("sidx3", 4, [P, 1], I32)
        dup3 = ring("dup3", 4, [P, 1])
        off3 = ring("off3", 4, [P, 1])
        def split(aps):
            return [b.rearrange("p (k d) -> p k d", k=2) for b in aps]

        al = split(views(0, 4, 2 * D, G_mem) + views(0, 4, 2 * D, R_mem))
        ssum, sr, sp, spT, xs = (split([b[:, q * 2 * C:(q + 1) * 2 * C] for b in node_mem]) for q in range(5))
        sx = [b[:, 10 * C:16 * C].rearrange("p (q k d) -> p q k d", q=3, k=2) for b in node_mem]
        stat4 = ring("stat4", 4, [P, 2, 6])
        mv4 = ring("mv4", 4, [P, 2, 2])
        tiny4 = ring("tiny4", 4, [P, 8, 2])

        s_load = sem("s_load")
        s_loadw = sem("s_loadw")
        s_zero = sem("s_zero")
        s_zero0 = sem("s_zero0")
        s_zero1 = sem("s_zero1")
        s_iota = sem("s_iota")
        s_const = sem("s_const")
        s_deg_hot = sem("s_deg_hot")
        s_deg_mm = sem("s_deg_mm")
        s_sqrt = sem("s_sqrt")
        s_srow = [sem(f"s_srow{i}") for i in range(4)]
        s_low = sem("s_low")
        s_hotT = sem("s_hotT")
        s_look = sem("s_look")
        s_pick = sem("s_pick")
        s_dis = sem("s_dis")
        s_coef = sem("s_coef")
        s_whi = sem("s_whi")
        s_wlo = sem("s_wlo")
        s_wres = sem("s_wres")
        s_wT = sem("s_wT")
        s_wTc = sem("s_wTc")
        s_wmv = sem("s_wmv")
        e_trow = [sem(f"e_trow{i}") for i in range(4)]
        e_gidx = sem("e_gidx")
        e_gather = [sem(f"e_gather{i}") for i in range(8)]
        e_M = sem("e_M")
        e_idx = sem("e_idx")
        e_mm = sem("e_mm")
        e_ev = sem("e_ev")
        e_scat = [sem(f"e_scat{i}") for i in range(8)]
        n_sl = [sem(f"n_sl{i}") for i in range(4)]
        n_xl = [sem(f"n_xl{i}") for i in range(8)]
        n_z = sem("n_z")
        n_hi = sem("n_hi")
        n_lo = sem("n_lo")
        n_tr = sem("n_tr")
        n_zT = sem("n_zT")
        n_mm = sem("n_mm")
        n_res = sem("n_res")
        n_rs = sem("n_rs")
        n_rstd = sem("n_rstd")
        n_x1 = sem("n_x1")
        n_st = [sem(f"n_st{i}") for i in range(4)]
        f_trow = [sem(f"f_trow{i}") for i in range(4)]
        f_fT = [sem(f"f_fT{i}") for i in range(4)]
        f_gidx = sem("f_gidx")
        f_gather = [sem(f"f_gather{i}") for i in range(4)]
        f_scaled = sem("f_scaled")
        f_proj = sem("f_proj")
        f_hi = sem("f_hi")
        f_lo = sem("f_lo")
        f_tr = sem("f_tr")
        f_hmm = sem("f_hmm")
        f_rawT = sem("f_rawT")
        f_soft = sem("f_soft")
        f_h = sem("f_h")
        f_wv = sem("f_wv")
        f_feat = sem("f_feat")
        f_m = sem("f_m")
        f_o = sem("f_o")
        f_us = sem("f_us")
        f_msg = sem("f_msg")
        f_M = sem("f_M")
        f_idx = sem("f_idx")
        f_mm = sem("f_mm")
        f_ev = sem("f_ev")
        f_scat = [sem(f"f_scat{i}") for i in range(4)]
        g_ss = [sem(f"g_ss{i}") for i in range(4)]
        g_al = [sem(f"g_al{i}") for i in range(8)]
        g_xs = [sem(f"g_xs{i}") for i in range(4)]
        g_soft = sem("g_soft")
        g_sr = sem("g_sr")
        g_sp = sem("g_sp")
        g_tr = sem("g_tr")
        g_spT = sem("g_spT")
        g_mm = sem("g_mm")
        g_res = sem("g_res")
        g_rs = sem("g_rs")
        g_rstd = sem("g_rstd")
        g_y = sem("g_y")
        g_st = [sem(f"g_st{i}") for i in range(8)]
        hold = {e: sem(f"hold_{e}") for e in ("pool", "sync", "vector", "scalar")}

        def held(eng, s, value):
            if not isinstance(value, int) or value > 0:
                name = {nc.gpsimd: "pool", nc.sync: "sync", nc.scalar: "scalar", nc.vector: "vector"}[eng]
                eng.wait_ge(s, value)
                eng.sem_inc(hold[name], 1)

        K_IDX = 3
        K_RES, K_ROOT = 4, 5
        K_PROJ, K_SOFT, K_PROD, K_MSG = 3, 4, 4, 3
        K_RES4, K_RSTD = 6, 4

        block = ctx.enter_context(nc.Block())

        @block.sync
        def _(sp_):
            for dst, src in ((src_i, src_cols), (dst_i, dst_cols), (ew, weight)):
                sp_.dma_start(dst[:, :], src).then_inc(s_load, 16)
            sp_.dma_start(rij[:, :, :], vec).then_inc(s_load, 16)

            for dst, src in (
                (b0_s[:, :], b0.broadcast_to([P, D])),
                (Wins[:, :], Win_s), (Winv[:, :], Win_v), (Wf1_s[:, :], Wf1),
                (bf1_c[:, :], bf1), (Wf2_s[:, :], Wf2[:, 0:512]), (bf2_c[:, :], bf2),
                (W1s_r[:, :, :], W1_s.rearrange("(f k) c -> f k c", k=2)),
                (W1v_r[:, :, :], W1_v.rearrange("(f k) c -> f k c", k=2)),
                (W2s_r[:, :], W2_s), (W2v_r[:, :], W2_v),
            ):
                sp_.dma_start(dst, src).then_inc(s_loadw, 16)

            for c in range(4):
                sp_.dma_start(W0_s[c], W0[c * P:(c + 1) * P, :]).then_inc(s_wres, 16)

            def edges0(s, u):
                held(sp_, s_low, s - 3)
                sp_.dma_start(srow[u][:, :], src_row[:, bass.ds(s * 256, 256)].broadcast_to([P, 256])) \
                   .then_inc(s_srow[u], 16)
                held(sp_, e_M, 2 * (s - 3))
                held(sp_, e_idx, 2 * K_IDX * (s - 3))
                sp_.dma_start(trow[u][:, :], dst_row[:, bass.ds(s * 256, 256)].broadcast_to([P, 256])) \
                   .then_inc(e_trow[u], 16)

            skewed(sp_, edges0, 0, 4, steps=T2)

            for k in range(8):
                sp_.wait_ge(e_scat[k], 16 * (T // 8))

            def nodes0(s, u):
                a = u % 4
                if live(s, 0):
                    held(sp_, n_hi, s - 3)
                    held(sp_, n_lo, s - 3)
                    sp_.dma_start(sl[a], rows(sum0, s)).then_inc(n_sl[a], 16)
                    held(sp_, n_res, K_RES * (s - 7))
                    sp_.dma_start(xl[u], rows(x, s)).then_inc(n_xl[u], 16)
                if live(s, 8):
                    t = s - 8
                    held(sp_, n_x1, t + 1)
                    sp_.dma_start(rows(x1_d, t), res[a]).then_inc(n_st[a], 16)
                    sp_.dma_start(sum1[bass.ds(t * P, P), C:D], res[a][:, C:D]).then_inc(n_st[a], 16)

            skewed(sp_, nodes0, 8, 8, unroll=8)

            def edges1(s, u):
                if live(s, 0):
                    held(sp_, f_hmm, s - 3)
                    sp_.dma_start(fT[u][:, :], rbf[:, bass.ds(s * P, P)]).then_inc(f_fT[u], 16)
                    held(sp_, f_M, s - 3)
                    held(sp_, f_idx, K_IDX * (s - 3))
                    sp_.dma_start(trow3[u][:, :], src_row[:, bass.ds(s * P, P)].broadcast_to([P, P])) \
                       .then_inc(f_trow[u], 16)

            skewed(sp_, edges1, 0, 4)

            for u in range(4):
                sp_.wait_ge(f_scat[u], 16 * (T // 4))

            def nodes1(s, u):
                if live(s, 0, T2):
                    a = u % 4
                    held(sp_, g_soft, 3 * (s - 3))
                    held(sp_, g_sr, s - 3)
                    sp_.dma_start(ssum[a], pair_rows(sum1, s, 0, C)).then_inc(g_ss[a], 16)
                if live(s, 7, T2):
                    t, b = s - 7, (u - 7) % 8
                    held(sp_, g_y, 2 * (t + 1))
                    sp_.dma_start(pair_rows(out, t, 0, D), al[b]).then_inc(g_st[b], 16)
                if live(s, 1, T2):
                    t, a, b = s - 1, (u - 1) % 4, (u - 1) % 8
                    held(sp_, g_st[b], 16 * turn(t, b, 8))
                    sp_.dma_start(al[b][:, :, C:D], pair_rows(sum1, t, C, D)).then_inc(g_al[b], 16)
                    held(sp_, g_res, K_RES4 * (t - 3))
                    sp_.dma_start(xs[a], pair_rows(x1_d, t, 0, C)).then_inc(g_xs[a], 16)

            skewed(sp_, nodes1, 7, 16, unroll=8, steps=T2)
            for v in range(8):
                sp_.wait_ge(g_st[v], 16 * (T2 // 8))

        @block.gpsimd
        def _(pool):
            pool.iota(iota_i[:, :], [[1, 256]], base=0, channel_multiplier=0).then_inc(s_iota, 1)
            pool.iota(lane_i[:, :], [[P, 2]], base=0, channel_multiplier=1).then_inc(s_iota, 1)
            pool.iota(ident_i[:, :], [[1, P]], base=0, channel_multiplier=-1).then_inc(s_iota, 1)
            pool.iota(trash_i[:, :], [[0, T // 2], [P, 2]], base=NP, channel_multiplier=1).then_inc(s_iota, 1)

            pool.wait_ge(s_whi, 4)
            for c in range(4):
                pool.tensor_tensor(W0l[:, c, :], W0_s[c], W0h[:, c, :].bitcast(F32), ALU.subtract).then_inc(s_wlo, 1)

            def edges0(s, u):
                if live(s, 0, T2):
                    for k in (2 * u, 2 * u + 1):
                        held(pool, e_gidx, 2 * s + (k - 2 * u) + 1)
                        held(pool, e_mm, s - 3)
                        pool.indirect_dma_start(G[k][:, :], None, x, bass.IndirectOffsetOnAxis(ap=gidx[k][:, :], axis=0)) \
                            .then_inc(e_gather[k], 16)
                if isinstance(s, int) and s == 3:
                    held(pool, s_zero0, 16 * 41)
                if live(s, 3, T2):
                    g, a = s - 3, (u - 3) % 4
                    for v in range(2):
                        k = 2 * a + v
                        held(pool, e_idx, 2 * K_IDX * g + 2 * K_IDX - 1 + v)
                        held(pool, e_ev, 2 * g + v + 1)
                        if v == 0:
                            for q in range(2):
                                held(pool, e_scat[2 * ((a - 1) % 4) + q], 16 * (turn(g, a, 4) + (a > 0)))
                        pool.indirect_dma_start(sum0, bass.IndirectOffsetOnAxis(ap=sidx[k][:, :], axis=0), R[k][:, :], None,
                                                compute_op=ALU.add).then_inc(e_scat[k], 16)

            skewed(pool, edges0, 3, 8, steps=T2)

            def nodes0(s, u):
                if live(s, 6):
                    t, w, mean, var = s - 6, tiny[(u - 6) % 4], mv[(u - 6) % 4][:, 0:1], mv[(u - 6) % 4][:, 1:2]
                    st = Stage(n_rstd, t, K_ROOT)
                    held(pool, n_res, K_RES * (t + 1))
                    st.mark(pool.tensor_scalar(w[:, 0:1], var, EPS, None, ALU.add))
                    held(pool, n_rstd, st.reached())
                    held(pool, n_rs, 2 * (t + 1))
                    st.mark(pool.tensor_scalar(w[:, 3:4], w[:, 2:3], w[:, 2:3], w[:, 0:1], ALU.mult, ALU.mult))
                    held(pool, n_rstd, st.reached())
                    st.mark(pool.tensor_scalar(w[:, 4:5], w[:, 3:4], -0.5, 1.5, ALU.mult, ALU.add))
                    st.settle(pool)
                    st.mark(pool.tensor_tensor(w[:, 5:6], w[:, 4:5], w[:, 2:3], ALU.mult))
                    held(pool, n_rstd, st.reached())
                    st.mark(pool.tensor_scalar(w[:, 6:7], mean, w[:, 5:6], -1.0, ALU.mult, ALU.mult))
                if live(s, 0):
                    pool.wait_ge(n_hi, s + 1)
                    wait(pool, n_tr, s - 3)
                    pool.tensor_tensor(z_lo[u][:, :], sl[u], z_hi[u][:, :].bitcast(F32), ALU.subtract).then_inc(n_lo, 1)

            skewed(pool, nodes0, 6, 8)

            for u in range(4):
                held(pool, n_st[u], 32 * (T // 4))
            held(pool, s_zero1, 16 * (T2 + 2))

            def edges1(s, u):
                if live(s, 7):
                    t, a = s - 7, (u - 7) % 4
                    pool.wait_ge(f_hi, t + 1)
                    wait(pool, f_mm, t - 3)
                    pool.tensor_tensor(msg_lo[a][:, :], msg[a % 2][:, P:640], msg_hi[a][:, :].bitcast(F32), ALU.subtract) \
                        .then_inc(f_lo, 1)
                if live(s, 1):
                    t, a = s - 1, (u - 1) % 4
                    held(pool, f_gidx, t + 1)
                    held(pool, f_tr, t - 3)
                    held(pool, f_proj, K_PROJ * (t - 3))
                    pool.indirect_dma_start(G3[a][:, :], None, x1_d, bass.IndirectOffsetOnAxis(ap=gidx3[a][:, :], axis=0)) \
                        .then_inc(f_gather[a], 16)
                if live(s, 9):
                    t, a = s - 9, (u - 9) % 4
                    held(pool, f_idx, K_IDX * (t + 1))
                    held(pool, f_ev, t + 1)
                    held(pool, f_scat[a - 1], 16 * (turn(t, a, 4) + (a > 0)))
                    pool.indirect_dma_start(sum1, bass.IndirectOffsetOnAxis(ap=sidx3[a][:, :], axis=0), R3[a][:, :], None,
                                            compute_op=ALU.add).then_inc(f_scat[a], 16)

            skewed(pool, edges1, 9, 12)

        @block.scalar
        def _(act):
            act.wait_ge(s_zero, 1)
            with act.Fori(0, 41) as j:
                act.dma_start(sum0[bass.ds(j * 256, 256), :].rearrange("(p r) d -> p (r d)", r=2), zeros[:, :]) \
                   .then_inc(s_zero0, 16)
            act.wait_ge(s_wres, 64)
            for c in range(4):
                act.copy(W0h[:, c, :], W0_s[c]).then_inc(s_whi, 1)
            act.wait_ge(s_const, 11)
            act.activation(degs[:, :], degm[:, :], ACT.Sqrt).then_inc(s_sqrt, 1)
            act.activation(rn[:, :], rsq[:, :, 0], ACT.Sqrt).then_inc(s_sqrt, 1)

            act.wait_ge(s_wT, 1)
            act.copy(W1vT[:, :, :], bank[7][:, 0:256].rearrange("p (k c) -> p k c", k=2)).then_inc(s_wTc, 1)
            act.wait_ge(s_wmv, 1)
            act.mul(MV[:, 0, :], bank[7][:, 256:384], 1.0 / (16.0 * C)).then_inc(s_wTc, 1)
            act.mul(MV[:, 1, :], bank[7][:, 384:512], Y0 / (16.0 * C)).then_inc(s_wTc, 1)

            def edges0(s, u):
                if live(s, 2, T2):
                    g, a = s - 2, (u - 2) % 4
                    for v in range(2):
                        k = 2 * a + v
                        act.wait_ge(e_mm, g + 1)
                        wait(act, e_scat[k], 16 * turn(g, a, 4))
                        act.copy(R[k][:, :], bank[2 * (a % 2) + v][:, :]).then_inc(e_ev, 1)
                    act.dma_start(sum1[bass.ds(g * 2 * P, 2 * P), 0:C].rearrange("(p r) d -> p r d", r=2),
                                  zeros[:, 0:2 * C].rearrange("p (r d) -> p r d", r=2)).then_inc(s_zero1, 16)

            skewed(act, edges0, 2, 8, steps=T2)
            for q in range(2):
                act.dma_start(sum1[NP + q * P:NP + (q + 1) * P, :], zeros[:, 0:D]).then_inc(s_zero1, 16)

            act.preload_act_table_set("natural_log_exp_and_others")

            def nodes0(s, u):
                if live(s, 5):
                    t, a = s - 5, (u - 5) % 4
                    act.wait_ge(n_res, K_RES * (t + 1))
                    act.activation(tiny[a][:, 1:2], mv[a][:, 1:2], ACT.Ln, bias=eps_c[:, :]).then_inc(n_rs, 1)
                if live(s, 2):
                    b = u % 2
                    act.wait_ge(n_tr, s - 1)
                    wait(act, n_mm, s - 3)
                    act.copy(zT_hi[b][:, :], bank[b][:, :]).then_inc(n_zT, 1)
                if live(s, 5):
                    act.wait_ge(n_rs, 2 * t + 1)
                    act.activation(tiny[a][:, 2:3], tiny[a][:, 1:2], ACT.Exp, scale=-0.5).then_inc(n_rs, 1)
                if live(s, 2):
                    act.copy(zT_lo[b][:, :], bank[2 + b][:, :]).then_inc(n_zT, 1)
                if live(s, 0):
                    a = u % 4
                    act.wait_ge(n_z, s + 1)
                    wait(act, n_tr, s - 3)
                    wait(act, n_lo, s - 3)
                    act.copy(z_hi[a][:, :], sl[a]).then_inc(n_hi, 1)
                if live(s, 6):
                    t, a = s - 6, (u - 6) % 4
                    act.wait_ge(n_rstd, K_ROOT * (t + 1))
                    act.activation(res[a], res[a], ACT.Identity, bias=tiny[a][:, 6:7], scale=tiny[a][:, 5:6]) \
                       .then_inc(n_x1, 1)

            skewed(act, nodes0, 6, 8, unroll=8)

            def edges1(s, u):
                if live(s, 4):
                    t, b = s - 4, u % 2
                    act.wait_ge(f_tr, t + 1)
                    wait(act, f_wv, t - 1)
                    act.copy(rawT[b][:, 0:512], bank[0][:, :]).then_inc(f_rawT, 1)
                    act.wait_ge(f_hmm, t + 1)
                    act.copy(rawT[b][:, 512:640], bank[1][:, 0:P]).then_inc(f_rawT, 1)
                    wait(act, f_h, t - 1)
                    st = Stage(f_soft, t, K_SOFT)
                    st.mark(act.activation(hx[b][:, 0, :], bank[1][:, P:2 * P], ACT.Abs, bias=bf1_c[:, :]))
                    st.mark(act.activation(hr[b][:, :], bank[1][:, P:2 * P], ACT.Relu, bias=bf1_c[:, :]))
                    st.settle(act)
                    st.mark(act.activation(hx[b][:, 1, :], hx[b][:, 0, :], ACT.Exp, scale=-1.0))
                    st.settle(act)
                    st.mark(act.activation(hx[b][:, 2, :], hx[b][:, 1, :], ACT.Ln, bias=1.0))
                if live(s, 5):
                    t, b = s - 5, (u - 5) % 2
                    act.wait_ge(f_wv, t + 1)
                    wait(act, f_m, K_PROD * (t - 1))
                    act.copy(feat[b][:, 0:512], bank[2][:, :]).then_inc(f_feat, 1)
                    act.copy(feat[b][:, 512:640], bank[3][:, 0:P]).then_inc(f_feat, 1)
                if live(s, 6):
                    t, b = s - 6, u % 2
                    act.wait_ge(f_o, t + 1)
                    wait(act, f_lo, t - 1)
                    act.copy(msg[b][:, 0:256], bank[5][:, 0:256]).then_inc(f_us, 1)
                if live(s, 7):
                    t, a = s - 7, (u - 7) % 4
                    act.wait_ge(f_msg, K_MSG * (t + 1))
                    wait(act, f_mm, t - 3)
                    act.copy(msg_hi[a][:, :], msg[a % 2][:, P:640]).then_inc(f_hi, 1)
                if live(s, 8):
                    t, a = s - 8, u % 4
                    act.wait_ge(f_mm, t + 1)
                    wait(act, f_scat[a], 16 * turn(t, a, 4))
                    act.copy(R3[a][:, :], bank[7][:, :]).then_inc(f_ev, 1)
                if live(s, 2):
                    t, a = s - 2, (u - 2) % 4
                    held(act, f_gather[a], 16 * (turn(t, a, 4) + 1))
                    act.activation(G3[a][:, :], G3[a][:, :], ACT.Identity, scale=ew[:, bass.ds(t, 1)]).then_inc(f_scaled, 1)

            skewed(act, edges1, 8, 12)

            def nodes1(s, u):
                t, a, b = s - 5, (u - 5) % 4, (u - 5) % 8
                u = u % 4
                st = Stage(g_soft, s, 3)
                def normalise(k):
                    act.activation(al[b][:, k, :], al[b][:, k, :], ACT.Identity, bias=tiny4[a][:, 6, k:k + 1],
                                   scale=tiny4[a][:, 5, k:k + 1]).then_inc(g_y, 1)

                if live(s, 2, T2):
                    t2, c = s - 2, (u - 2) % 4
                    act.wait_ge(g_tr, t2 + 1)
                    wait(act, g_mm, t2 - 3)
                    act.copy(spT[c][:, :, :], bank[c][:, 0:256].rearrange("p (k c) -> p k c", k=2)).then_inc(g_spT, 1)
                if live(s, 0, T2):
                    act.wait_ge(g_ss[u], 16 * (turn(s, u, 4) + 1))
                    wait(act, g_sp, s - 3)
                    st.mark(act.activation(sx[u][:, 0, :, :], ssum[u][:, :, :], ACT.Abs))
                if live(s, 4, T2):
                    t4 = s - 4
                    act.wait_ge(g_res, K_RES4 * (t4 + 1))
                    act.activation(tiny4[u][:, 1, :], tiny4[u][:, 0, :], ACT.Ln).then_inc(g_rs, 1)
                if live(s, 5, T2):
                    act.wait_ge(g_rstd, K_RSTD * (t + 1))
                    normalise(0)
                if live(s, 0, T2):
                    st.settle(act)
                    st.mark(act.activation(sx[u][:, 1, :, :], sx[u][:, 0, :, :], ACT.Exp, scale=-1.0))
                if live(s, 4, T2):
                    act.wait_ge(g_rs, 2 * t4 + 1)
                    act.activation(tiny4[u][:, 2, :], tiny4[u][:, 1, :], ACT.Exp, scale=-0.5).then_inc(g_rs, 1)
                if live(s, 5, T2):
                    normalise(1)
                if live(s, 0, T2):
                    st.settle(act)
                    st.mark(act.activation(sx[u][:, 2, :, :], sx[u][:, 1, :, :], ACT.Ln, bias=1.0))

            skewed(act, nodes1, 5, 8, unroll=8, steps=T2)
        @block.vector
        def _(dve):
            count = [0]

            def link(ins):
                count[0] += 1
                ins.then_inc(s_const, 1)
                dve.wait_ge(s_const, count[0])

            dve.memset(zeros[:, :], 0.0).then_inc(s_zero, 1)
            dve.memset(eps_c[:, :], EPS)
            dve.wait_ge(s_iota, 4)
            dve.tensor_copy(iota_f[:, :], iota_i[:, :])
            dve.tensor_copy(lane[:, :], lane_i[:, :])
            dve.tensor_copy(trash[:, :], trash_i[:, :])
            dve.wait_ge(s_load, 64)
            dve.tensor_copy(src_f[:, :], src_i[:, :])
            dve.tensor_copy(dst_f[:, :], dst_i[:, :])
            dve.tensor_scalar(part_i[:, 0, :], dst_i[:, :], 127, None, ALU.bitwise_and)
            dve.tensor_scalar(part_i[:, 1, :], dst_i[:, :], 7, None, ALU.logical_shift_right)
            dve.tensor_scalar(part_i[:, 2, :], src_i[:, :], 127, None, ALU.bitwise_and)
            dve.tensor_scalar(part_i[:, 3, :], src_i[:, :], 7, None, ALU.logical_shift_right)
            dve.tensor_scalar(ident_r[:, :], ident_i[:, :], 0.0, None, ALU.is_equal)
            link(dve.tensor_scalar(ident[:, :], ident_i[:, :], 0.0, None, ALU.is_equal))
            dve.tensor_tensor(to_trash_src[:, :], trash[:, :], src_f[:, :], ALU.subtract)
            dve.tensor_tensor(to_trash_dst[:, :], trash[:, :], dst_f[:, :], ALU.subtract)
            for u in range(2):
                dve.tensor_scalar(before[:, u, :], iota_f[:, :], lane[:, u:u + 1], None, ALU.is_lt)
            link(dve.tensor_copy(part[:, :, :], part_i[:, :, :]))

            def hots(t, u):
                wait(dve, s_deg_mm, t - 2)
                dve.tensor_scalar(hot_lo[u][:, :], iota_f[:, 0:P], part[:, 0, bass.ds(t, 1)], None, ALU.is_equal) \
                   .then_inc(s_deg_hot, 1)
                dve.tensor_scalar(hot_hi[u][:, :], iota_f[:, 0:T], part[:, 1, bass.ds(t, 1)], ew[:, bass.ds(t, 1)],
                                  ALU.is_equal, ALU.mult).then_inc(s_deg_hot, 1)

            skewed(dve, hots, 0, 4)

            dve.tensor_tensor(rsq[:, :, :], rij[:, :, :], rij[:, :, :], ALU.mult)
            dve.wait_ge(s_deg_mm, T + 1)
            link(dve.tensor_scalar(deg[:, :], bank[6][:, 0:T], 1.0, None, ALU.add))
            link(dve.tensor_scalar(degm[:, :], deg[:, :], 1e-34, None, ALU.max))
            link(dve.tensor_scalar(deg[:, :], deg[:, :], 0.0, None, ALU.is_gt))
            link(dve.tensor_tensor(rsq[:, :, 0], rsq[:, :, 0], rsq[:, :, 1], ALU.add))
            link(dve.tensor_tensor(rsq[:, :, 0], rsq[:, :, 0], rsq[:, :, 2], ALU.add))
            for q in range(2):
                k = Y0 / (16.0 * C ** 0.5) if q == 0 else 1.0 / (16.0 * C ** 0.5 * 3.0 ** 0.5)
                dve.wait_ge(s_loadw, 16 * 11)
                link(dve.tensor_scalar(W1s_s[:, q, :], W1s_r[:, q, :], k, None, ALU.mult))
            link(dve.tensor_scalar(W2s_s[:, :], W2s_r[:, :], 1.0 / C ** 0.5, None, ALU.mult))
            link(dve.tensor_copy(degt[:, :], degm[:, :]))
            dve.wait_ge(s_sqrt, 2)
            link(dve.reciprocal(dis[:, :], degs[:, :]))
            link(dve.reciprocal(rn[:, :], rn[:, :]))
            link(dve.tensor_tensor(degt[:, :], degt[:, :], dis[:, :], ALU.mult))
            link(dve.tensor_tensor(degt[:, :], degt[:, :], dis[:, :], ALU.mult))
            link(dve.tensor_scalar(degt[:, :], degt[:, :], -0.5, 1.5, ALU.mult, ALU.add))
            link(dve.tensor_tensor(dis[:, :], dis[:, :], degt[:, :], ALU.mult))
            link(dve.tensor_tensor(dis[:, :], dis[:, :], deg[:, :], ALU.mult))
            link(dve.scalar_tensor_tensor(Y[:, :, :], rij[:, :, :], Y1, rn[:, :].unsqueeze(2).broadcast_to([P, T, 3]),
                                          ALU.mult, ALU.mult))
            dve.sem_inc(s_dis, 1)

            def edges0(s, u):
                if live(s, 0, T2):
                    for v in range(2):
                        k = 2 * u + v
                        wait(dve, e_gather[k], 16 * turn(s, u, 4))
                        dve.tensor_scalar(gidx[k][:, :], src_i[:, bass.ds(2 * s + v, 1)], 0.0, None, ALU.add).then_inc(e_gidx, 1)
                    dve.wait_ge(s_srow[u], 16 * (turn(s, u, 4) + 1))
                    wait(dve, s_hotT, s - 3)
                    dve.tensor_scalar(slow[u][:, :], srow[u][:, :], 127, None, ALU.bitwise_and).then_inc(s_low, 1)
                if live(s, 1, T2):
                    g, a, b = s - 1, (u - 1) % 4, (u - 1) % 2
                    dve.wait_ge(s_look, g + 1)
                    for v in range(2):
                        t = 2 * g + v
                        dve.scalar_tensor_tensor(junk80[:, 2 * a + v, :], iota_f[:, 0:T], part[:, 3, bass.ds(t, 1)],
                                                 bank[4 + b][:, v * T:(v + 1) * T], ALU.is_equal, ALU.mult,
                                                 accum_out=dsrc[:, bass.ds(t, 1)]).then_inc(s_pick, 1)
                if live(s, 0, T2):
                    dve.wait_ge(s_low, s + 1)
                    wait(dve, s_look, s - 3)
                    dve.tensor_scalar(hotT[u][:, :], slow[u][:, :], lane[:, 0:1], None, ALU.is_equal).then_inc(s_hotT, 1)
                if live(s, 1, T2):
                    dve.wait_ge(s_pick, 2 * (g + 1))
                    dve.tensor_tensor(coef[:, bass.ds(2 * g, 2)], ew[:, bass.ds(2 * g, 2)], dsrc[:, bass.ds(2 * g, 2)],
                                      ALU.mult).then_inc(s_coef, 1)
                    dve.wait_ge(e_trow[a], 16 * (turn(g, a, 4) + 1))
                    st = Stage(e_idx, g, 2 * K_IDX)
                    for v in range(2):
                        k, t = 2 * a + v, 2 * g + v
                        st.mark(dve.scalar_tensor_tensor(junk[k][:, :], trow[a][:, :], dst_f[:, bass.ds(t, 1)], before[:, v, :],
                                                         ALU.is_equal, ALU.mult, accum_out=dup[k][:, :]))
                    dve.wait_ge(s_coef, g + 1)
                    for v in range(2):
                        k, t = 2 * a + v, 2 * g + v
                        wait(dve, e_mm, g - 3)
                        dve.tensor_scalar(M[k][:, :], trow[a][:, :], dst_f[:, bass.ds(t, 1)], coef[:, bass.ds(t, 1)],
                                          ALU.is_equal, ALU.mult).then_inc(e_M, 1)
                    for v in range(2):
                        k, t = 2 * a + v, 2 * g + v
                        if v == 0:
                            st.settle(dve)
                        st.mark(dve.tensor_scalar(off[k][:, :], dup[k][:, :], 1.0, to_trash_dst[:, bass.ds(t, 1)], ALU.min, ALU.mult))
                    st.settle(dve)
                    for v in range(2):
                        k, t = 2 * a + v, 2 * g + v
                        wait(dve, e_scat[k], 16 * turn(g, a, 4))
                        st.mark(dve.tensor_scalar(sidx[k][:, :], off[k][:, :], dst_f[:, bass.ds(t, 1)], None, ALU.add))

            skewed(dve, edges0, 1, 8, steps=T2)

            def nodes0(s, u):
                if live(s, 4):
                    t, a = s - 4, (u - 4) % 4
                    st = Stage(n_res, t, K_RES)
                    dve.wait_ge(n_mm, t + 1)
                    wait(dve, n_st[a], 32 * turn(t, a, 4))
                    st.mark(dve.scalar_tensor_tensor(res[a], bank[4 + a][:, :], dis[:, bass.ds(t, 1)], b0_s[:, :],
                                                     ALU.mult, ALU.add))
                if live(s, 0):
                    c = u % 4
                    dve.wait_ge(n_sl[c], 16 * (turn(s, c, 4) + 1))
                    dve.wait_ge(n_xl[u], 16 * (turn(s, u, 8) + 1))
                    dve.scalar_tensor_tensor(sl[c], xl[u], dis[:, bass.ds(s, 1)], sl[c], ALU.mult, ALU.add).then_inc(n_z, 1)
                if live(s, 4):
                    st.settle(dve)
                    st.mark(dve.scalar_tensor_tensor(res[a], res[a], 0.0, xl[(u - 4) % 8], ALU.max, ALU.add))
                    st.settle(dve)
                    st.mark(dve.bn_stats(stat[a][:, :], res[a]))
                    held(dve, n_res, st.reached())
                    st.mark(dve.bn_aggr(mv[a][:, :], stat[a][:, :]))

            skewed(dve, nodes0, 4, 8, unroll=8)

            def edges1(s, u):
                if live(s, 0):
                    wait(dve, f_gather[u], 16 * turn(s, u, 4))
                    dve.tensor_scalar(gidx3[u][:, :], dst_i[:, bass.ds(s, 1)], 0.0, None, ALU.add).then_inc(f_gidx, 1)
                t, a = s - 3, (u - 3) % 4
                sj = Stage(f_proj, t, K_PROJ)
                gv = G3[a][:, C:D].rearrange("p (c i) -> p c i", i=3)
                tm, b = s - 7, (u - 7) % 4
                si = Stage(f_idx, tm, K_IDX)
                if live(s, 3):
                    dve.wait_ge(f_scaled, t + 1)
                    wait(dve, f_tr, t - 3)
                    sj.mark(dve.tensor_scalar(proj[a][:, :], gv[:, :, 0], Y[:, bass.ds(t, 1), 0], None, ALU.mult))
                if live(s, 7):
                    dve.wait_ge(f_trow[b], 16 * (turn(tm, b, 4) + 1))
                    si.mark(dve.scalar_tensor_tensor(junk3[b][:, :], trow3[b][:, :], src_f[:, bass.ds(tm, 1)],
                                                     before[:, 0, 0:P], ALU.is_equal, ALU.mult, accum_out=dup3[b][:, :]))
                if live(s, 3):
                    sj.settle(dve)
                    sj.mark(dve.scalar_tensor_tensor(proj[a][:, :], gv[:, :, 1], Y[:, bass.ds(t, 1), 1], proj[a][:, :],
                                                     ALU.mult, ALU.add))
                if live(s, 7):
                    wait(dve, f_mm, tm - 3)
                    dve.tensor_scalar(M3[b][:, :], trow3[b][:, :], src_f[:, bass.ds(tm, 1)], None,
                                      ALU.is_equal).then_inc(f_M, 1)
                if live(s, 3):
                    sj.settle(dve)
                    sj.mark(dve.scalar_tensor_tensor(proj[a][:, :], gv[:, :, 2], Y[:, bass.ds(t, 1), 2], proj[a][:, :],
                                                     ALU.mult, ALU.add))
                if live(s, 7):
                    si.settle(dve)
                    si.mark(dve.tensor_scalar(off3[b][:, :], dup3[b][:, :], 1.0, to_trash_src[:, bass.ds(tm, 1)],
                                              ALU.min, ALU.mult))
                if live(s, 4):
                    t, c = s - 4, u % 2
                    wait(dve, f_wv, t - 1)
                    dve.wait_ge(f_soft, K_SOFT * (t + 1))
                    dve.scalar_tensor_tensor(h[c][:, :], hx[c][:, 2, :], -LOG2, hr[c][:, :], ALU.add, ALU.add).then_inc(f_h, 1)
                if live(s, 7):
                    si.settle(dve)
                    wait(dve, f_scat[b], 16 * turn(tm, b, 4))
                    si.mark(dve.tensor_scalar(sidx3[b][:, :], off3[b][:, :], src_f[:, bass.ds(tm, 1)], None, ALU.add))
                if live(s, 5):
                    t, c = s - 5, (u - 5) % 2
                    dve.wait_ge(f_wv, t + 1)
                    dve.wait_ge(f_feat, 2 * (t + 1))
                    wait(dve, f_o, t - 1)
                    st = Stage(f_m, t, K_PROD)
                    f_s, f_z = feat[c][:, 512:640], feat[c][:, 384:512]
                    for q, fe in ((0, f_s), (1, f_z), (2, f_s)):
                        st.mark(dve.scalar_tensor_tensor(m[c][:, q * P:(q + 1) * P], bank[4][:, q * P:(q + 1) * P],
                                                         bf2_c[:, q:q + 1], fe, ALU.add, ALU.mult))
                    st.mark(dve.scalar_tensor_tensor(
                        m[c][:, 384:768].rearrange("p (i e) -> p i e", i=3),
                        bank[4][:, 384:512].unsqueeze(1).broadcast_to([P, 3, P]), bf2_c[:, 3:4],
                        feat[c][:, 0:384].rearrange("p (i e) -> p i e", i=3), ALU.add, ALU.mult))
                if live(s, 6):
                    t, c = s - 6, u % 2
                    dve.wait_ge(f_us, t + 1)
                    dve.wait_ge(f_o, t + 1)
                    st = Stage(f_msg, t, K_MSG)
                    mo = msg[c][:, 256:640].rearrange("p (c i) -> p c i", i=3)
                    for i in range(3):
                        st.mark(dve.scalar_tensor_tensor(mo[:, :, i], msg[c][:, 0:P], Y[:, bass.ds(t, 1), i],
                                                         bank[6][:, i * P:(i + 1) * P], ALU.mult, ALU.add))

            skewed(dve, edges1, 7, 12)

            def nodes1(s, u):
                b3, u = (u - 3) % 8, u % 4
                t5, a5 = s - 5, (u - 5) % 4
                w = tiny4[a5]
                sv = Stage(g_rstd, t5, K_RSTD)
                t1, a1 = s - 1, (u - 1) % 4
                t3, a3 = s - 3, (u - 3) % 4
                st = Stage(g_res, t3, K_RES4)
                if live(s, 5, T2):
                    dve.wait_ge(g_rs, 2 * (t5 + 1))
                    sv.mark(dve.scalar_tensor_tensor(w[:, 3, :], w[:, 2, :], -0.5, w[:, 2, :], ALU.mult, ALU.mult))
                if live(s, 0, T2):
                    dve.wait_ge(g_ss[u], 16 * (turn(s, u, 4) + 1))
                    dve.tensor_scalar(sr[u][:, :, :], ssum[u][:, :, :], 0.0, -LOG2, ALU.max, ALU.add).then_inc(g_sr, 1)
                if live(s, 5, T2):
                    sv.settle(dve)
                    sv.mark(dve.tensor_tensor(w[:, 4, :], w[:, 3, :], w[:, 0, :], ALU.mult))
                if live(s, 1, T2):
                    dve.wait_ge(g_sr, t1 + 1)
                    dve.wait_ge(g_soft, 3 * (t1 + 1))
                    wait(dve, g_tr, t1 - 3)
                    dve.tensor_tensor(sp[a1][:, :, :], sr[a1][:, :, :], sx[a1][:, 2, :, :], ALU.add).then_inc(g_sp, 1)
                if live(s, 5, T2):
                    sv.settle(dve)
                    sv.mark(dve.scalar_tensor_tensor(w[:, 5, :], w[:, 4, :], 1.5, w[:, 2, :], ALU.add, ALU.mult))
                if live(s, 3, T2):
                    dve.wait_ge(g_mm, t3 + 1)
                    dve.wait_ge(g_xs[a3], 16 * (turn(t3, a3, 4) + 1))
                    dve.wait_ge(g_al[b3], 16 * (turn(t3, b3, 8) + 1))
                    st.mark(dve.tensor_tensor(al[b3][:, :, 0:C], bank[4 + a3][:, 0:256].rearrange("p (k c) -> p k c", k=2),
                                              xs[a3][:, :, :], ALU.add))
                if live(s, 5, T2):
                    sv.settle(dve)
                    sv.mark(dve.scalar_tensor_tensor(w[:, 6, :], mv4[a5][:, :, 0], -1.0, w[:, 5, :], ALU.mult, ALU.mult))
                if live(s, 3, T2):
                    st.settle(dve)
                    for k in range(2):
                        st.mark(dve.bn_stats(stat4[a3][:, k, :], al[b3][:, k, :]))
                    held(dve, g_y, 2 * (t3 - 3))
                    held(dve, g_res, st.reached())
                    for k in range(2):
                        st.mark(dve.bn_aggr(mv4[a3][:, k, :], stat4[a3][:, k, :]))
                    st.settle(dve)
                    st.mark(dve.tensor_scalar(tiny4[a3][:, 0, :], mv4[a3][:, :, 1], EPS, None, ALU.add))

            skewed(dve, nodes1, 5, 8, unroll=8, steps=T2)

        @block.tensor
        def _(pe):
            pe.wait_ge(s_zero, 1)
            pe.matmul(bank[6][:, 0:T], zeros[:, 0:P], zeros[:, 0:T], start=True, stop=False,
                      skip_group_check=True).then_inc(s_deg_mm, 1)

            def deg_mm(t, u):
                pe.wait_ge(s_deg_hot, 2 * t + 2)
                pe.matmul(bank[6][:, 0:T], hot_lo[u][:, :], hot_hi[u][:, :], start=False, stop=False,
                          skip_group_check=True).then_inc(s_deg_mm, 1)

            skewed(pe, deg_mm, 0, 4)

            pe.wait_ge(s_loadw, 16 * 11)
            pe.wait_ge(s_const, 2)
            for q in range(2):
                ins = pe.transpose(bank[7][:, q * P:(q + 1) * P], W1v_r[:, q, :], ident[:, :])
            ins.then_inc(s_wT, 1)
            pe.wait_ge(s_wTc, 1)
            for q in range(2):
                ins = pe.matmul(bank[7][:, 256 + q * P:256 + (q + 1) * P], W1vT[:, q, :], W2v_r[:, :], start=True, stop=True)
            ins.then_inc(s_wmv, 1)

            pe.wait_ge(s_dis, 1)

            def edges0(s, u):
                if live(s, 0, T2):
                    b = u % 2
                    pe.wait_ge(s_hotT, s + 1)
                    wait(pe, s_pick, 2 * (s - 1))
                    for v in range(2):
                        ins = pe.matmul(bank[4 + b][:, v * T:(v + 1) * T], hotT[u][:, v * P:(v + 1) * P], dis[:, :],
                                        start=True, stop=True)
                    ins.then_inc(s_look, 1)
                if live(s, 2, T2):
                    g, a, b = s - 2, (u - 2) % 4, u % 2
                    for v in range(2):
                        pe.wait_ge(e_gather[2 * a + v], 16 * (turn(g, a, 4) + 1))
                    pe.wait_ge(e_M, 2 * g + 2)
                    wait(pe, e_ev, 2 * (g - 1))
                    for v in range(2):
                        for q in range(2):
                            ins = pe.matmul(bank[2 * b + v][:, :], M[2 * a + q][:, v * P:(v + 1) * P], G[2 * a + q][:, :],
                                            start=(q == 0), stop=(q == 1))
                    ins.then_inc(e_mm, 1)

            skewed(pe, edges0, 2, 8, steps=T2)

            pe.wait_ge(e_ev, T)
            pe.wait_ge(s_pick, T)
            pe.wait_ge(s_wlo, 4)

            def nodes0(s, u):
                if live(s, 2):
                    t, a, b = s - 2, (u - 2) % 4, u % 2
                    pe.wait_ge(n_hi, t + 1)
                    wait(pe, n_zT, 2 * (t - 1))
                    for part_, to in ((z_hi, bank[b]), (z_lo, bank[2 + b])):
                        if part_ is z_lo:
                            pe.wait_ge(n_lo, t + 1)
                        for c in range(4):
                            ins = pe.matmul(to[:, c * P:(c + 1) * P], part_[a][:, c * P:(c + 1) * P], ident_r[:, :],
                                            start=True, stop=True)
                    ins.then_inc(n_tr, 1)
                if live(s, 3):
                    t, a, b = s - 3, (u - 3) % 4, (u - 3) % 2
                    pe.wait_ge(n_zT, 2 * (t + 1))
                    wait(pe, n_res, K_RES * (t - 3))
                    for c in range(4):
                        for k, (zt, w) in enumerate(((zT_hi, W0h), (zT_hi, W0l), (zT_lo, W0h))):
                            ins = pe.matmul(bank[4 + a][:, :], zt[b][:, c * P:(c + 1) * P], w[:, c, :],
                                            start=(c == 0 and k == 0), stop=(c == 3 and k == 2))
                    ins.then_inc(n_mm, 1)

            skewed(pe, nodes0, 3, 8)

            pe.wait_ge(n_zT, 2 * T)
            pe.wait_ge(n_res, K_RES * T)
            pe.wait_ge(s_wTc, 3)
            pe.wait_ge(s_const, 11)

            def edges1(s, u):
                if live(s, 4):
                    t, a = s - 4, u
                    pe.wait_ge(f_proj, K_PROJ * (t + 1))
                    pe.wait_ge(f_scaled, t + 1)
                    wait(pe, f_rawT, 2 * t)
                    wait(pe, f_soft, K_SOFT * t)
                    gv = G3[a][:, C:D].rearrange("p (c i) -> p c i", i=3)
                    for i in range(3):
                        pe.transpose(bank[0][:, i * P:(i + 1) * P], gv[:, :, i], ident[:, :])
                    pe.transpose(bank[0][:, 384:512], proj[a][:, :], ident[:, :])
                    pe.transpose(bank[1][:, 0:P], G3[a][:, 0:C], ident[:, :]).then_inc(f_tr, 1)
                    pe.wait_ge(f_fT[a], 16 * (turn(t, a, 4) + 1))
                    pe.matmul(bank[1][:, P:2 * P], Wf1_s[:, :], fT[a][:, :], start=True, stop=True).then_inc(f_hmm, 1)
                if live(s, 5):
                    t, b = s - 5, (u - 5) % 2
                    pe.wait_ge(f_rawT, 2 * (t + 1))
                    wait(pe, f_feat, 2 * t)
                    pe.matmul(bank[2][:, :], Winv[:, :], rawT[b][:, 0:512], start=True, stop=True)
                    pe.matmul(bank[3][:, 0:P], Wins[:, :], rawT[b][:, 512:640], start=True, stop=True)
                    pe.wait_ge(f_h, t + 1)
                    wait(pe, f_m, K_PROD * t)
                    for q in range(4):
                        base = 256 * (q // 2) + q % 2
                        ins = pe.matmul(bank[4][:, q * P:(q + 1) * P], Wf2_s[:, base:base + 255:2], h[b][:, :],
                                        start=True, stop=True)
                    ins.then_inc(f_wv, 1)
                if live(s, 6):
                    t, b = s - 6, u % 2
                    pe.wait_ge(f_m, K_PROD * (t + 1))
                    wait(pe, f_us, t)
                    wait(pe, f_msg, K_MSG * t)
                    pe.matmul(bank[5][:, 0:P], m[b][:, 256:384], MV[:, 0, :], start=True, stop=True)
                    for q in range(2):
                        pe.matmul(bank[5][:, P:2 * P], m[b][:, q * P:(q + 1) * P], W1s_s[:, q, :], start=(q == 0), stop=(q == 1))
                    for i in range(3):
                        ins = pe.matmul(bank[6][:, i * P:(i + 1) * P], m[b][:, (3 + i) * P:(4 + i) * P], MV[:, 1, :],
                                        start=True, stop=True)
                    ins.then_inc(f_o, 1)
                if live(s, 8):
                    t, a = s - 8, u % 4
                    pe.wait_ge(f_hi, t + 1)
                    pe.wait_ge(f_M, t + 1)
                    wait(pe, f_ev, t)
                    pe.matmul(bank[7][:, :], M3[a][:, :], msg_hi[a][:, :], start=True, stop=False)
                    pe.wait_ge(f_lo, t + 1)
                    pe.matmul(bank[7][:, :], M3[a][:, :], msg_lo[a][:, :], start=False, stop=True).then_inc(f_mm, 1)

            skewed(pe, edges1, 8, 12)

            pe.wait_ge(f_ev, T)

            def nodes1(s, u):
                if live(s, 1, T2):
                    t, a = s - 1, (u - 1) % 4
                    pe.wait_ge(g_sp, t + 1)
                    wait(pe, g_spT, t - 3)
                    for k in range(2):
                        ins = pe.transpose(bank[a][:, k * P:(k + 1) * P], sp[a][:, k, :], ident[:, :])
                    ins.then_inc(g_tr, 1)
                if live(s, 2, T2):
                    t, a = s - 2, (u - 2) % 4
                    pe.wait_ge(g_spT, t + 1)
                    wait(pe, g_res, K_RES4 * (t - 3))
                    for k in range(2):
                        ins = pe.matmul(bank[4 + a][:, k * C:(k + 1) * C], spT[a][:, k, :], W2s_s[:, :], start=True, stop=True)
                    ins.then_inc(g_mm, 1)

            skewed(pe, nodes1, 2, 8, steps=T2)


def kernel(x, src, dst, edge_attr_20, edge_attr_3, edge_weight, L0_gnn_W, L0_gnn_b, L1_gnn_W_in2f_s, L1_gnn_W_in2f_v,
           L1_gnn_Wf1, L1_gnn_bf1, L1_gnn_Wf2, L1_gnn_bf2, L1_gnn_W1_s, L1_gnn_W1_v, L1_gnn_W2_s, L1_gnn_W2_v):
    import concourse.bacc as bacc
    from concourse.bass_utils import run_bass_kernel_spmd

    def padded(a, value=0):
        a = np.asarray(a)
        out = np.full((NP,) + a.shape[1:], value, a.dtype)
        out[:N] = a
        return out

    def columns(a):
        return np.ascontiguousarray(np.moveaxis(a.reshape((T, P) + a.shape[1:]), 0, 1))

    ends = []
    for a in (src, dst):
        a = padded(a)
        a[N:] = np.arange(N, NP, dtype=a.dtype)
        ends.append(a)
    s, d = ends
    bf2 = np.asarray(L1_gnn_bf2)[:512].reshape(2, C, 2)
    arrays = {
        "x": padded(x),
        "src_cols": columns(s), "dst_cols": columns(d), "src_row": s.reshape(1, NP), "dst_row": d.reshape(1, NP),
        "weight": columns(padded(edge_weight)),
        "rbf": np.ascontiguousarray(padded(edge_attr_20).T),
        "vec": columns(padded(edge_attr_3, 1)),
        "W0": np.asarray(L0_gnn_W), "b0": np.asarray(L0_gnn_b).reshape(1, D),
        "Win_s": np.asarray(L1_gnn_W_in2f_s), "Win_v": np.asarray(L1_gnn_W_in2f_v),
        "Wf1": np.asarray(L1_gnn_Wf1), "bf1": np.asarray(L1_gnn_bf1).reshape(C, 1),
        "Wf2": np.asarray(L1_gnn_Wf2), "bf2": np.ascontiguousarray(bf2.transpose(1, 0, 2).reshape(C, 4)),
        "W1_s": np.asarray(L1_gnn_W1_s), "W1_v": np.asarray(L1_gnn_W1_v),
        "W2_s": np.asarray(L1_gnn_W2_s), "W2_v": np.asarray(L1_gnn_W2_v),
    }
    nc = bacc.Bacc("TRN2", target_bir_lowering=False, num_devices=1)
    args = [nc.dram_tensor(n, a.shape, mybir.dt.from_np(a.dtype), kind="ExternalInput").ap() for n, a in arrays.items()]
    args.append(nc.dram_tensor("out", (NP, D), F32, kind="ExternalOutput").ap())
    build(nc, *args)
    r = run_bass_kernel_spmd(nc, [arrays], core_ids=[0])
    return r.results[0]["out"][:N]
```
